# Optimizing a Trainium2 kernel written in Bass

```python
import numpy as np
import jax
import jax.numpy as jnp

def _softmax(x, axis=-1):
    return jax.nn.softmax(x, axis=axis)

def _gelu(x):
    return jax.nn.gelu(x, approximate=True)

def _silu(x):
    return jax.nn.silu(x)

def _sigmoid(x):
    return jax.nn.sigmoid(x)

def _layernorm(x, axis=-1, eps=1e-05):
    m = jnp.mean(x, axis=axis, keepdims=True)
    v = jnp.var(x, axis=axis, keepdims=True)
    return (x - m) / jnp.sqrt(v + eps)

def _scatter_add(tgt, idx, src, axis=0):
    return tgt.at[idx].add(src)

def _segment_sum(src, seg, n):
    return jax.ops.segment_sum(src, seg, n)
kernel_name = 'mk_prb_d1_jaxref_r4_dbcecd'

def setup_inputs(seed: int=0):
    np.random.seed(seed)
    _w = jnp.asarray

    def _L0_attn_setup():
        import jax, jax.numpy as jnp
        import numpy as np
        B, L, D_IN, D_OUT, H, WIN = (1, 512, 256, 256, 16, 64)
        D_H = D_OUT // H
        key = jax.random.key(seed)
        ks = jax.random.split(key, 5)
        s = 0.02
        return {'x': jax.random.normal(ks[0], (B, L, D_IN), dtype=jnp.float32), 'Wq': jax.random.normal(ks[1], (D_IN, D_OUT), dtype=jnp.float32) * s, 'Wk': jax.random.normal(ks[2], (D_IN, D_OUT), dtype=jnp.float32) * s, 'Wv': jax.random.normal(ks[3], (D_IN, D_OUT), dtype=jnp.float32) * s, 'Wo': jax.random.normal(ks[4], (D_OUT, D_IN), dtype=jnp.float32) * s}
    _L0_attn_in = _L0_attn_setup()

    def _L0_ffn_setup():
        import jax, jax.numpy as jnp
        import numpy as np
        EPS = 1e-06
        LN_EPS = 1e-05

        def _absmean_core(W):
            gamma = jnp.mean(jnp.abs(W)) + EPS
            Ws = W / gamma
            Wq = jnp.sign(Ws) * jnp.minimum(jnp.round(jnp.abs(Ws)), 1.0)
            return (Wq, gamma)

        @jax.custom_vjp
        def absmean(W):
            return _absmean_core(W)[0]

        def _absmean_fwd(W):
            Wq, gamma = _absmean_core(W)
            return (Wq, gamma)

        def _absmean_bwd(gamma, g):
            return (g / gamma,)
        absmean.defvjp(_absmean_fwd, _absmean_bwd)

        def layernorm(x, w, b, eps=LN_EPS):
            mu = jnp.mean(x, axis=-1, keepdims=True)
            var = jnp.mean((x - mu) ** 2, axis=-1, keepdims=True)
            return (x - mu) * jax.lax.rsqrt(var + eps) * w + b
        key = jax.random.key(seed)
        k1, k2, k3 = jax.random.split(key, 3)
        d, h = (256, 1024)
        B, T = (8, 512)
        return {'x': jax.random.normal(k1, (B, T, d), jnp.float32), 'W_fc': jax.random.normal(k2, (h, d), jnp.float32), 'ln_w': jnp.ones((h,), jnp.float32), 'ln_b': jnp.zeros((h,), jnp.float32), 'W_proj': jax.random.normal(k3, (d, h), jnp.float32)}
    _L0_ffn_in = _L0_ffn_setup()
    _d = {'L0_attn_x': _L0_attn_in['x'], 'L0_attn_Wq': _L0_attn_in['Wq'], 'L0_attn_Wk': _L0_attn_in['Wk'], 'L0_attn_Wv': _L0_attn_in['Wv'], 'L0_attn_Wo': _L0_attn_in['Wo'], 'L0_ffn_W_fc': _L0_ffn_in['W_fc'], 'L0_ffn_ln_w': _L0_ffn_in['ln_w'], 'L0_ffn_ln_b': _L0_ffn_in['ln_b'], 'L0_ffn_W_proj': _L0_ffn_in['W_proj']}
    _x0 = _d['L0_attn_x']
    _d['L0_attn_x'] = jax.random.normal(jax.random.fold_in(jax.random.key(seed), 1), (8, 512, 256), dtype=_x0.dtype)
    del _x0
    return _d

def reference(L0_attn_x, L0_attn_Wq, L0_attn_Wk, L0_attn_Wv, L0_attn_Wo, L0_ffn_W_fc, L0_ffn_ln_w, L0_ffn_ln_b, L0_ffn_W_proj):

    def _L0_attn_ref(x, Wq, Wk, Wv, Wo):
        import jax, jax.numpy as jnp
        import numpy as np
        B, L, D_IN, D_OUT, H, WIN = (1, 512, 256, 256, 16, 64)
        D_H = D_OUT // H
        Bx, Lx, _ = x.shape
        W = min(WIN, Lx)
        scale = D_H ** (-0.5)

        def split_heads(t):
            return t.reshape(Bx, Lx, H, D_H).transpose(0, 2, 1, 3)
        q = split_heads(x @ Wq)
        k = split_heads(x @ Wk)
        v = split_heads(x @ Wv)
        offsets = jnp.arange(W) - (W - 1)
        idx = jnp.arange(Lx)[:, None] + offsets[None, :]
        invalid = idx < 0
        idx = jnp.clip(idx, 0, Lx - 1)
        k_win = jnp.take(k, idx, axis=2)
        v_win = jnp.take(v, idx, axis=2)
        scores = jnp.einsum('bhld,bhlwd->bhlw', q, k_win) * scale
        scores = jnp.where(invalid[None, None, :, :], -jnp.inf, scores)
        attn = jax.nn.softmax(scores, axis=-1)
        ctx = jnp.einsum('bhlw,bhlwd->bhld', attn, v_win)
        ctx = ctx.transpose(0, 2, 1, 3).reshape(Bx, Lx, D_OUT)
        return ctx @ Wo

    def _L0_ffn_ref(x, W_fc, ln_w, ln_b, W_proj):
        import jax, jax.numpy as jnp
        import numpy as np
        EPS = 1e-06
        LN_EPS = 1e-05

        def _absmean_core(W):
            gamma = jnp.mean(jnp.abs(W)) + EPS
            Ws = W / gamma
            Wq = jnp.sign(Ws) * jnp.minimum(jnp.round(jnp.abs(Ws)), 1.0)
            return (Wq, gamma)

        @jax.custom_vjp
        def absmean(W):
            return _absmean_core(W)[0]

        def _absmean_fwd(W):
            Wq, gamma = _absmean_core(W)
            return (Wq, gamma)

        def _absmean_bwd(gamma, g):
            return (g / gamma,)
        absmean.defvjp(_absmean_fwd, _absmean_bwd)

        def layernorm(x, w, b, eps=LN_EPS):
            mu = jnp.mean(x, axis=-1, keepdims=True)
            var = jnp.mean((x - mu) ** 2, axis=-1, keepdims=True)
            return (x - mu) * jax.lax.rsqrt(var + eps) * w + b
        h = jnp.einsum('btd,hd->bth', x, absmean(W_fc))
        h = jax.nn.gelu(h, approximate=False)
        h = layernorm(h, ln_w, ln_b)
        return jnp.einsum('bth,dh->btd', h, absmean(W_proj))
    x = L0_attn_x
    xn = _layernorm(x, axis=-1)
    x = x + _L0_attn_ref(xn, L0_attn_Wq, L0_attn_Wk, L0_attn_Wv, L0_attn_Wo) + _L0_ffn_ref(xn, L0_ffn_W_fc, L0_ffn_ln_w, L0_ffn_ln_b, L0_ffn_W_proj)
    return x

_drawn_inputs = setup_inputs


def setup_inputs(seed=0):
    import zlib

    import numpy as np

    out = dict(_drawn_inputs(seed))
    spreads = {'L0_ffn_ln_w': (1.0, 0.2), 'L0_ffn_ln_b': (0.0, 0.1)}
    factors = {'L0_attn_Wq': 8.0, 'L0_attn_Wk': 8.0, 'L0_attn_Wv': 8.0, 'L0_attn_Wo': 8.0}
    for name, (base, spread) in spreads.items():
        noise = np.random.default_rng([zlib.crc32(name.encode()), seed]).standard_normal(out[name].shape)
        drawn = base * np.exp(spread * noise) if base else spread * noise
        out[name] = jnp.asarray(drawn.astype(out[name].dtype))
    for name, factor in factors.items():
        out[name] = (out[name] * factor).astype(out[name].dtype)
    return out
```

```python
import concourse.bass as bass
from concourse import mybir
from contextlib import ExitStack


def attention_and_ternary_ffn(
    nc: bass.Bass,
    x: bass.AP,
    w_q: bass.AP,
    w_k: bass.AP,
    w_v: bass.AP,
    w_o: bass.AP,
    w_fc: bass.AP,
    ln_w: bass.AP,
    ln_b: bass.AP,
    w_proj: bass.AP,
    out: bass.AP,
):
    fp32 = mybir.dt.float32
    fp16 = mybir.dt.float16
    bf16 = mybir.dt.bfloat16
    u32 = mybir.dt.uint32
    ALU = mybir.AluOpType
    ACT = mybir.ActivationFunctionType
    AX = mybir.AxisListType

    P = 128
    NB, L, D = x.shape
    HID = w_fc.shape[1]
    H = 16
    DH = D // H
    W = 64
    NT = L // P
    KD = D // P
    NH = HID // P
    NF = NH // 2
    NJ = L // W
    NP = H // 2
    HALF = NJ // 2
    VC = 2 * DH + 1
    LN_EPS = 1e-5
    EPS = 1e-6
    NEG = -1e38
    SMALLEST = 2.0 ** -100

    ctx = ExitStack()
    with ctx:
        def sb(name, shape, dt):
            return ctx.enter_context(nc.sbuf_tensor(name, shape, dt))

        def sem(name):
            return ctx.enter_context(nc.semaphore(name))

        x_in = sb("x_in", [P, NT, D], fp32)
        w_raw = sb("w_raw", [P, 4, KD, D], fp32)
        w_hi = sb("w_hi", [P, 4, KD, D], fp16)
        w_lo = sb("w_lo", [P, 4, KD, D], fp16)
        fc_t = sb("fc_t", [P, KD, HID], fp16)
        proj_t = sb("proj_t", [P, NH, D], fp16)
        lnw = sb("lnw", [P, NH], fp32)
        lnb = sb("lnb", [P, NH], fp32)
        lnw_s = sb("lnw_s", [P, NH], fp32)
        red = sb("red", [P, 8], fp32)
        redall = sb("redall", [P, 8], fp32)
        pow2 = sb("pow2", [P, 5], fp32)
        inv2 = sb("inv2", [P, 5], fp32)
        theta = sb("theta", [P, 2], fp32)
        ntheta = sb("ntheta", [P, 2], fp32)
        exp_scale = sb("exp_scale", [P, 1], fp32)
        attn_scale = sb("attn_scale", [P, 1], fp32)
        crow = sb("crow", [1, 2 * D], fp32)
        csum = sb("csum", [P, 2, D], fp32)
        ident = sb("ident", [P, P], fp32)
        ones = sb("ones", [P, P], fp32)
        expo = sb("expo", [P, NT], fp32)
        onehot = sb("onehot", [P, P], bf16)
        mask_q = sb("mask_q", [P, 2, 4, P], bf16)
        mask_k = sb("mask_k", [P, 2, P], bf16)
        bn6 = sb("bn6", [P, NT, 6], fp32)
        mv = sb("mv", [P, NT, 2], fp32)
        veps = sb("veps", [P, NT], fp32)
        rstd = sb("rstd", [P, NT], fp32)
        xn = sb("xn", [P, NT, D], fp32)
        res = sb("res", [P, NT, D], fp32)
        xt_hi = sb("xt_hi", [P, KD, L], fp16)
        xt_lo = sb("xt_lo", [P, KD, L], fp16)
        qk_split = sb("qk_split", [P, 2, KD, 2, L], fp16)
        q_stack = sb("q_stack", [P, NP, NJ, P], fp16)
        k_stack = sb("k_stack", [P, NP, W + L], fp16)
        v_even = sb("v_even", [P, NT, NP, VC], fp32)
        v_odd = sb("v_odd", [P, NT, NP, VC], fp32)
        gel = sb("gel", [P, NF, 2, L], fp32)
        gsq = sb("gsq", [P, NF, 2, L], fp32)
        fc_raw = gel[:, 0:NF // 2].rearrange("p i a n -> p (i a n)").rearrange("p (k n) -> p k n", k=KD)
        proj_raw = gel[:, NF // 2:NF].rearrange("p i a n -> p (i a n)").rearrange("p (k n) -> p k n", k=NH)
        proj_t32 = gsq[:, 0:NF // 2].rearrange("p i a n -> p (i a n)").rearrange("p (k n) -> p k n", k=NH)
        below = gsq[:, NF // 2:NF].rearrange("p i a n -> p (i a n)").bitcast(fp16)[:, 0:NH * D]
        gsum = sb("gsum", [P, 2, 2, L], fp32)
        g_hi = sb("g_hi", [P, NH, L], fp16)
        g_lo = sb("g_lo", [P, NH, L], fp16)
        negmax = sb("negmax", [P, NJ, NP], fp32)
        mt = sb("mt", [4 * NP, 2, 3, P], bf16)
        mt_left = sb("mt_left", [4 * NP, 2, 2, P], fp32)
        shift = sb("shift", [P, NJ, NP * P], bf16)
        probs = sb("probs", [P, 3, NP, P], fp32)
        rden = sb("rden", [P, NJ, NP], fp32)
        ctxn = sb("ctxn", [P, NJ, NP, DH], fp32)
        ct_hi = sb("ct_hi", [P, 2, L], fp16)
        ct_lo = sb("ct_lo", [P, 2, L], fp16)
        moments = sb("moments", [P, NT, 2], fp32)
        msq = sb("msq", [P, NT], fp32)
        var2 = sb("var2", [P, NT], fp32)
        rstd2 = sb("rstd2", [P, NT], fp32)
        rs2 = sb("rs2", [P, NT], fp32)
        nrm2 = sb("nrm2", [P, NT], fp32)
        y_ffn = sb("y_ffn", [P, NT, D], fp32)
        y_out = sb("y_out", [P, NT, D], fp32)
        y_tmp = sb("y_tmp", [P, NT, D], fp32)

        scratch = nc.dram_tensor("qk_scratch", [2, 2, D, L], fp16, kind="Internal").ap()

        big = [ctx.enter_context(nc.psum_tensor(f"big{i}", [P, 2, 512], fp32)) for i in range(3)]
        small = [ctx.enter_context(nc.psum_tensor(f"small{i}", [P, 512], fp32)) for i in range(2)]

        PER = {}

        AHEAD = ("exp_ready", "y_ready", "proj_added", "stored")

        def event(name, per, unit=1):
            s = sem(name)
            PER[name] = (s, per * unit, unit)
            return name

        x_loaded = event("x_loaded", 1, 16)
        scratch_written = [event(f"scratch_written{s}", 2, 16) for s in range(2)]
        stacks_loaded = event("stacks_loaded", 16, 16)
        v_shifted = event("v_shifted", 2, 16)
        shift_loaded = [event(f"shift_loaded{h}", 3, 16) for h in range(2)]
        stored = event("stored", NT, 16)
        xt_done = event("xt_done", 1)
        qk_done = event("qk_done", 2)
        v_done = event("v_done", 1)
        fc_done = event("fc_done", NF)
        sa_done = event("sa_done", NJ)
        mt_done = event("mt_done", 2)
        mom_done = event("mom_done", 1)
        proj_done = event("proj_done", NT)
        st_done = event("st_done", NJ)
        pv_done = event("pv_done", NJ)
        ct_done = event("ct_done", 2)
        wo_done = event("wo_done", NT)
        xt_hi_ready = event("xt_hi_ready", 1)
        qk_hi_ready = event("qk_hi_ready", 2)
        v_ready = event("v_ready", 1)
        gelu_ready = event("gelu_ready", NF)
        square_ready = event("square_ready", NF)
        exp_ready = event("exp_ready", NJ)
        ct_hi_ready = event("ct_hi_ready", 2)
        xn_ready = event("xn_ready", 1)
        veps_ready = event("veps_ready", 1)
        xt_ready = event("xt_ready", 1)
        qk_ready = event("qk_ready", 2)
        g_hi_ready = event("g_hi_ready", NH)
        g_ready = event("g_ready", NH)
        max_ready = event("max_ready", NJ)
        mt_ready = event("mt_ready", 2)
        moments_ready = event("moments_ready", 1)
        var_ready = event("var_ready", 1)
        proj_added = event("proj_added", NT)
        ffn_ready = event("ffn_ready", NT)
        rden_ready = event("rden_ready", NJ)
        ctx_ready = event("ctx_ready", NJ)
        ct_ready = event("ct_ready", 2)
        y_ready = event("y_ready", NT)
        STEPS = 25
        dve_step = event("dve_step", STEPS)
        res_ready = event("res_ready", 1)
        rstd_ready = event("rstd_ready", 1)
        rstd2_ready = event("rstd2_ready", 1)
        SUMS = 2 * (NF - 1)
        sum_ready = event("sum_ready", SUMS)
        w_loaded = sem("w_loaded")
        fc_loaded = sem("fc_loaded")
        ln_loaded = sem("ln_loaded")
        pool_const = sem("pool_const")
        consts_ready = sem("consts_ready")
        dve_pre = sem("dve_pre")
        red_ready = sem("red_ready")
        red_done = sem("red_done")
        crow_done = sem("crow_done")
        crow_ready = sem("crow_ready")
        csum_done = sem("csum_done")
        weights_ready = sem("weights_ready")
        proj_t_ready = sem("proj_t_ready")
        csum_ready = sem("csum_ready")

        def wait(eng, b, name, n):
            s, per, unit = PER[name]
            eng.wait_ge(s, b * per + (n * unit + (name in AHEAD)))

        def sig(name):
            return PER[name][0], PER[name][2]

        READ_OUT = {"xt": xt_ready, "qk": qk_ready, "v": v_ready, "fc": gelu_ready, "sa": max_ready,
                    "mt": mt_ready, "mom": moments_ready, "proj": proj_added, "st": exp_ready,
                    "pv": ctx_ready, "ct": ct_ready, "wo": y_ready}
        ORDER = [("xt", 0), ("qk", 0), ("qk", 1), ("v", 0), ("fc", 0), ("fc", 1), ("fc", 2), ("fc", 3),
                 ("sa", 0), ("sa", 1), ("sa", 2), ("sa", 3), ("mom", 0), ("proj", 0), ("mt", 0),
                 ("sa", 4), ("sa", 5), ("proj", 1), ("sa", 6), ("sa", 7), ("proj", 2), ("mt", 1),
                 ("st", 0), ("st", 1), ("proj", 3), ("st", 2), ("pv", 0), ("st", 3), ("pv", 1), ("st", 4), ("pv", 2),
                 ("st", 5), ("pv", 3), ("st", 6), ("pv", 4), ("ct", 0), ("st", 7), ("pv", 5), ("pv", 6),
                 ("pv", 7), ("ct", 1), ("wo", 0), ("wo", 1), ("wo", 2), ("wo", 3)]
        BIG = ("xt", "qk", "v", "fc", "sa", "st")
        slot, before = {}, {}
        for ring, kinds in ((big, True), (small, False)):
            jobs = [j for j in ORDER if (j[0] in BIG) == kinds]
            for i, j in enumerate(jobs):
                slot[j] = ring[i % len(ring)]
            for r in range(len(ring)):
                users = jobs[r::len(ring)]
                for i, j in enumerate(users):
                    before[j] = users[i - 1] if i else None

        def wait_slot(eng, b, job):
            prev = before[job]
            if prev is not None:
                wait(eng, b, READ_OUT[prev[0]], prev[1] + 1)
            else:
                last = [j for j in ORDER if slot[j] is slot[job]][-1]
                assert READ_OUT[last[0]] in AHEAD
                wait(eng, b, READ_OUT[last[0]], 0)

        block = ctx.enter_context(nc.Block())

        @block.sync
        def _(sp):
            sp.dma_start(x_in[:], x[0].rearrange("(t p) d -> p t d", p=P)).then_inc(PER[x_loaded][0], 16)
            for i, w in enumerate((w_q, w_k, w_v, w_o)):
                sp.dma_start(w_raw[:, i], w.rearrange("(k p) n -> p k n", p=P)).then_inc(w_loaded, 16)
            sp.dma_start(lnw[:], ln_w).then_inc(ln_loaded, 16)
            sp.dma_start(lnb[:], ln_b).then_inc(ln_loaded, 16)
            sp.dma_start(fc_raw, w_fc.rearrange("(k p) n -> p k n", p=P)).then_inc(fc_loaded, 16)
            sp.dma_start(proj_raw, w_proj.rearrange("(k p) n -> p k n", p=P)).then_inc(fc_loaded, 16)
            sp.wait_ge(consts_ready, 1)
            sp.sem_inc(PER[stored][0], 1)
            with sp.Fori(0, NB) as b:
                nxt = (b + 1) % NB
                for v in (nxt * (L * D) * 4, b * (L * D) * 4, b * 2 + 1, b * 2 + 2, b + 1, b * 32 + 32,
                          b * NT + 2, b * NT + 3, b * NT + 4, b * NT + 5):
                    sp.compute_val(v)
                sp.wait_ge(PER[res_ready][0], b + 1)
                sp.wait_ge(PER[xn_ready][0], b + 1)
                sp.dma_start(x_in[:], x[nxt].rearrange("(t p) d -> p t d", p=P)).then_inc(PER[x_loaded][0], 16)
                for s in range(2):
                    for part, ready in enumerate((qk_hi_ready, qk_ready)):
                        sp.wait_ge(PER[ready][0], b * 2 + s + 1)
                        sp.dma_start(scratch[s, part].rearrange("(k p) n -> p k n", p=P),
                                     qk_split[:, s, :, part]).then_inc(PER[scratch_written[s]][0], 16)
                for s in range(2):
                    sp.wait_ge(PER[scratch_written[s]][0], b * 32 + 32)
                    for half in range(2):
                        for a in range(2):
                            for c in range(2):
                                r = half * 4 * DH + (a * 2 + c) * DH
                                part = a if s == 0 else c
                                src = scratch[s, part].rearrange("(u d i) n -> u d i n", u=2, d=DH)[half]
                                if s == 0:
                                    src = src.rearrange("d i (j q) -> d (i j) q", q=W)
                                    dst = q_stack[r:r + DH].rearrange("p i j (u q) -> p (i j) u q", u=2)[:, :, half]
                                else:
                                    dst = k_stack[r:r + DH, :, W:]
                                sp.dma_start(dst, src).then_inc(PER[stacks_loaded][0], 16)
                sp.wait_ge(PER[v_ready][0], b + 1)
                sp.dma_start(v_odd[0:W, 1:NT], v_even[W:P, 0:NT - 1]).then_inc(PER[v_shifted][0], 16)
                sp.dma_start(v_odd[W:P, :], v_even[0:W, :]).then_inc(PER[v_shifted][0], 16)
                for h in range(2):
                    sp.wait_ge(PER[mt_ready][0], b * 2 + h + 1)
                    for c in range(3):
                        sp.dma_start(shift[W + c:W + c + 1, h * HALF:(h + 1) * HALF, :], mt[:, h, c, :]).then_inc(
                            PER[shift_loaded[h]][0], 16)
                for t in range(NT):
                    wait(sp, b, y_ready, t + 1)
                    sp.dma_start(out[b, t * P:(t + 1) * P, :], y_out[:, t]).then_inc(PER[stored][0], 16)
            sp.wait_ge(PER[stored][0], NB * NT * 16 + 1)

        @block.gpsimd
        def _(pool):
            g = nc.gpsimd
            steps = [0]

            def step(ins):
                steps[0] += 1
                ins.then_inc(pool_const, 1)
                pool.wait_ge(pool_const, steps[0])

            step(g.memset(ident[:], 0.0))
            step(g.memset(ones[:], 1.0))
            step(g.memset(expo[:], -0.5))
            step(g.memset(onehot[:], 0.0))
            step(g.memset(mask_q[:], 0.0))
            step(g.memset(mask_k[:], 0.0))
            step(g.affine_select(out=ident[:], in_=ident[:], compare_op=ALU.not_equal, fill=1.0, base=0,
                                 pattern=[[1, P]], channel_multiplier=-1))
            oh = onehot[:].rearrange("p (a q) -> p a q", q=W)
            step(g.affine_select(out=oh, in_=oh, compare_op=ALU.not_equal, fill=1.0, base=0,
                                 pattern=[[0, 2], [1, W]], channel_multiplier=-1))
            for m in (mask_q[0:W].rearrange("p f u k -> p (f u) k"), mask_k[0:W]):
                n = m.shape[1]
                step(g.affine_select(out=m, in_=m, compare_op=ALU.is_gt, fill=NEG, base=0,
                                     pattern=[[0, n], [1, P]], channel_multiplier=-1))
                step(g.affine_select(out=m, in_=m, compare_op=ALU.is_ge, fill=NEG, base=W,
                                     pattern=[[0, n], [-1, P]], channel_multiplier=1))
            step(g.memset(mask_q[0:W, 1, :, 0:W], NEG))
            step(g.memset(mask_k[0:W, 1, 0:W], NEG))
            step(g.memset(mask_k[W:W + 3, :, :], 1.0))
            step(g.memset(shift[:].bitcast(u32), 0))
            sh = shift[:].rearrange("p j (u q) -> p (j u) q", q=W)
            step(g.affine_select(out=sh, in_=sh, compare_op=ALU.not_equal, fill=1.0, base=0,
                                 pattern=[[0, NJ * H], [1, W]], channel_multiplier=-1))
            step(g.memset(q_stack[:].bitcast(u32), 0))
            step(g.memset(k_stack[:, :, 0:W].bitcast(u32), 0))
            step(g.memset(v_odd[0:W, 0], 0.0))
            g.memset(v_even[:, :, :, 2 * DH:], 1.0).then_inc(consts_ready, 1)
            pool.wait_ge(red_ready, 1)
            g.partition_all_reduce(redall[:, 0:5], red[:, 0:5], P, bass.bass_isa.ReduceOp.max).then_inc(red_done, 1)
            g.partition_all_reduce(redall[:, 5:7], red[:, 5:7], P, bass.bass_isa.ReduceOp.add).then_inc(red_done, 1)
            pool.wait_ge(PER[veps_ready][0], 1)
            g.tensor_tensor(rstd[:], veps[:], expo[:], ALU.pow).then_inc(*sig(rstd_ready))
            pool.wait_ge(csum_ready, 1)
            with pool.Fori(0, NB) as b:
                for v in (b * 16 + 16, b + 1, b * NT + 1, b * NF + 2, b * NF + 3, b * NF + 4, b * SUMS + 1, b * SUMS + 2,
                          b * SUMS + 3, b * SUMS + 4, b + 2):
                    pool.compute_val(v)
                pool.wait_ge(PER[x_loaded][0], b * 16 + 16)
                wait(pool, b, proj_added, 0)
                g.tensor_tensor(res[:], x_in[:], csum[:, 1:2, :].broadcast_to([P, NT, D]), ALU.add).then_inc(
                    *sig(res_ready))
                for i in range(1, NF):
                    for kind, src, ready in ((0, gel, gelu_ready), (1, gsq, square_ready)):
                        pool.wait_ge(PER[ready][0], b * NF + i + 1)
                        if i > 1:
                            pool.wait_ge(PER[sum_ready][0], b * SUMS + 2 * (i - 1) + kind - 1)
                        first = src[:, 0] if i == 1 else gsum[:, kind]
                        g.tensor_tensor(gsum[:, kind], first, src[:, i], ALU.add).then_inc(*sig(sum_ready))
                pool.wait_ge(PER[var_ready][0], b + 1)
                g.tensor_tensor(rstd2[:], var2[:], expo[:], ALU.pow).then_inc(*sig(rstd2_ready))
                pool.wait_ge(PER[veps_ready][0], b + 2)
                g.tensor_tensor(rstd[:], veps[:], expo[:], ALU.pow).then_inc(*sig(rstd_ready))

        @block.scalar
        def _(act):
            s = nc.scalar
            act.sem_inc(PER[exp_ready][0], 1)
            with act.Fori(0, NB) as b:
                wait(act, b, xt_done, 1)
                s.activation(xt_hi[:], slot["xt", 0][:], ACT.Copy).then_inc(*sig(xt_hi_ready))
                for i in range(2):
                    wait(act, b, qk_done, i + 1)
                    s.activation(qk_split[:, i, :, 0, :], slot["qk", i][:], ACT.Copy).then_inc(*sig(qk_hi_ready))
                wait(act, b, v_done, 1)
                s.activation(v_even[:, :, :, 0:2 * DH],
                             slot["v", 0][:].rearrange("p k (t i d) -> p (k t) i d", i=NP, d=2 * DH),
                             ACT.Copy).then_inc(*sig(v_ready))
                for i in range(NF):
                    wait(act, b, fc_done, i + 1)
                    s.activation(gel[:, i], slot["fc", i][:], ACT.Gelu).then_inc(*sig(gelu_ready))
                    wait(act, b, gelu_ready, i + 1)
                    s.activation(gsq[:, i], gel[:, i], ACT.Square).then_inc(*sig(square_ready))

                def exp(j):
                    wait(act, b, st_done, j + 1)
                    if j >= 3:
                        wait(act, b, pv_done, j - 2)
                    s.activation(probs[:, j % 3], slot["st", j][:].rearrange("p a (u n) -> p (a u) n", n=P),
                                 ACT.Exp, scale=exp_scale[:, 0:1]).then_inc(*sig(exp_ready))

                def ct(h):
                    wait(act, b, ct_done, h + 1)
                    s.activation(ct_hi[:].rearrange("p u (j q) -> p j u q", q=W)[:, h * HALF:(h + 1) * HALF],
                                 slot["ct", h][:].rearrange("p (j u q) -> p j u q", u=2, q=W),
                                 ACT.Copy).then_inc(*sig(ct_hi_ready))

                for j in range(NJ):
                    exp(j)
                    if j == 6:
                        ct(0)
                ct(1)

        @block.vector
        def _(dve):
            v = nc.vector
            pre = [0]

            def link_pre(ins):
                pre[0] += 1
                ins.then_inc(dve_pre, 1)
                dve.wait_ge(dve_pre, pre[0])

            def statistics(link):
                for t in range(NT):
                    last = v.bn_stats(bn6[:, t], x_in[:, t])
                link(last)
                v.memset(veps[:], 0.0)
                for t in range(NT):
                    last = v.bn_aggr(mv[:, t], bn6[:, t])
                link(last)
                v.tensor_scalar(veps[:], mv[:, :, 1], LN_EPS, None, ALU.add).then_inc(*sig(veps_ready))

            def normalize():
                for t in range(NT):
                    last = v.tensor_scalar(xn[:, t], x_in[:, t], mv[:, t, 0:1], rstd[:, t:t + 1],
                                           ALU.subtract, ALU.mult)
                last.then_inc(*sig(xn_ready))

            dve.wait_ge(PER[x_loaded][0], 16)
            statistics(link_pre)
            dve.wait_ge(w_loaded, 64)
            v.tensor_reduce(red[:, 0:4], w_raw[:].rearrange("p a k n -> p a (k n)"), AX.X, ALU.max,
                            apply_absolute_value=True)
            dve.wait_ge(ln_loaded, 32)
            v.tensor_reduce(red[:, 4:5], lnw[:], AX.X, ALU.max, apply_absolute_value=True)
            dve.wait_ge(fc_loaded, 32)
            v.tensor_reduce(red[:, 5:6], fc_raw.rearrange("p k n -> p (k n)"), AX.X, ALU.add,
                            apply_absolute_value=True)
            v.tensor_reduce(red[:, 6:7], proj_raw.rearrange("p k n -> p (k n)"), AX.X, ALU.add,
                            apply_absolute_value=True).then_inc(red_ready, 1)
            dve.wait_ge(PER[rstd_ready][0], 1)
            normalize()
            dve.wait_ge(red_done, 2)
            link_pre(v.tensor_scalar(red[:, 0:5], redall[:, 0:5], SMALLEST, None, ALU.max))
            link_pre(v.tensor_scalar(pow2[:].bitcast(u32), red[:, 0:5].bitcast(u32), 0x7F800000, None,
                                     ALU.bitwise_and))
            v.reciprocal(inv2[:], pow2[:])
            link_pre(v.tensor_scalar(red[:, 5:7], redall[:, 5:7], 1.0 / (D * HID), EPS, ALU.mult, ALU.add))
            v.tensor_scalar(theta[:], red[:, 5:7], 0.5, None, ALU.mult)
            v.tensor_scalar(ntheta[:], red[:, 5:7], -0.5, None, ALU.mult)
            v.tensor_scalar(exp_scale[:], pow2[:, 0:1], pow2[:, 1:2], DH ** -0.5, ALU.mult, ALU.mult)
            link_pre(v.tensor_scalar(attn_scale[:], pow2[:, 2:3], pow2[:, 3:4], None, ALU.mult))
            for i in range(4):
                last = v.tensor_scalar(w_hi[:, i], w_raw[:, i], inv2[:, i:i + 1], None, ALU.mult)
            link_pre(last)
            for i in range(4):
                last = v.scalar_tensor_tensor(out=w_lo[:, i], in0=w_raw[:, i], scalar=inv2[:, i:i + 1],
                                              in1=w_hi[:, i], op0=ALU.mult, op1=ALU.subtract)
            v.tensor_scalar(lnw_s[:], lnw[:], inv2[:, 4:5], None, ALU.mult)
            bl = below.rearrange("p (k n) -> p k n", k=KD)
            link_pre(v.tensor_scalar(bl, fc_raw, ntheta[:, 0:1], None, ALU.is_lt))
            link_pre(v.scalar_tensor_tensor(out=fc_t[:], in0=fc_raw, scalar=theta[:, 0:1], in1=bl,
                                            op0=ALU.is_gt, op1=ALU.subtract))
            bl = below.rearrange("p (k n) -> p k n", k=NH)
            link_pre(v.tensor_scalar(bl, proj_raw, ntheta[:, 1:2], None, ALU.is_lt))
            v.scalar_tensor_tensor(out=proj_t32, in0=proj_raw, scalar=theta[:, 1:2], in1=bl,
                                   op0=ALU.is_gt, op1=ALU.subtract).then_inc(proj_t_ready, 1)
            dve.wait_ge(proj_t_ready, 1)
            v.tensor_copy(proj_t[:], proj_t32).then_inc(weights_ready, 1)
            dve.wait_ge(crow_done, 1)
            v.tensor_copy(crow[:], small[0][0:1, :]).then_inc(crow_ready, 1)
            dve.wait_ge(csum_done, 1)
            v.tensor_copy(csum[:].rearrange("p a n -> p (a n)"), small[1][:]).then_inc(csum_ready, 1)

            dve.sem_inc(PER[y_ready][0], 1)
            dve.sem_inc(PER[proj_added][0], 1)
            with dve.Fori(0, NB) as b:
                n_step = [0]

                def link(ins):
                    n_step[0] += 1
                    ins.then_inc(*sig(dve_step))
                    wait(dve, b, dve_step, n_step[0])

                wait(dve, b, xt_hi_ready, 1)
                v.tensor_tensor(xt_lo[:], slot["xt", 0][:], xt_hi[:], ALU.subtract).then_inc(*sig(xt_ready))
                for i in range(2):
                    wait(dve, b, qk_hi_ready, i + 1)
                    v.tensor_tensor(qk_split[:, i, :, 1, :], slot["qk", i][:], qk_split[:, i, :, 0, :],
                                    ALU.subtract).then_inc(*sig(qk_ready))

                def split_gelu(i):
                    wait(dve, b, gelu_ready, i + 1)
                    for a in range(2):
                        v.tensor_scalar(g_hi[:, 2 * i + a], gel[:, i, a], lnw_s[:, 2 * i + a:2 * i + a + 1], None,
                                        ALU.mult).then_inc(*sig(g_hi_ready))
                    for a in range(2):
                        wait(dve, b, g_hi_ready, 2 * i + a + 1)
                        v.scalar_tensor_tensor(out=g_lo[:, 2 * i + a], in0=gel[:, i, a],
                                               scalar=lnw_s[:, 2 * i + a:2 * i + a + 1], in1=g_hi[:, 2 * i + a],
                                               op0=ALU.mult, op1=ALU.subtract).then_inc(*sig(g_ready))

                def maximum(j):
                    wait(dve, b, sa_done, j + 1)
                    v.tensor_reduce(negmax[:, j], slot["sa", j][:].rearrange("p a (u k) -> p (a u) k", k=P),
                                    AX.X, ALU.max, negate=True).then_inc(*sig(max_ready))

                def split_maxima(h):
                    wait(dve, b, mt_done, h + 1)
                    row = slot["mt", h][0:4 * NP, 0:P]
                    link(v.tensor_copy(mt[:, h, 0], row))
                    link(v.tensor_tensor(mt_left[:, h, 0], row, mt[:, h, 0], ALU.subtract))
                    link(v.tensor_copy(mt[:, h, 1], mt_left[:, h, 0]))
                    v.tensor_tensor(mt[:, h, 2], mt_left[:, h, 0], mt[:, h, 1], ALU.subtract).then_inc(*sig(mt_ready))

                def hidden_moments():
                    wait(dve, b, mom_done, 1)
                    v.tensor_scalar(moments[:], slot["mom", 0][:, 0:2 * NT].rearrange("p (t a) -> p t a", a=2),
                                    1.0 / HID, None, ALU.mult).then_inc(*sig(moments_ready))
                    wait(dve, b, moments_ready, 1)
                    link(v.tensor_tensor(msq[:], moments[:, :, 0], moments[:, :, 0], ALU.mult))
                    link(v.tensor_tensor(var2[:], moments[:, :, 1], msq[:], ALU.subtract))
                    v.tensor_scalar(var2[:], var2[:], 0.0, LN_EPS, ALU.max, ALU.add).then_inc(*sig(var_ready))

                def hidden_scales():
                    wait(dve, b, rstd2_ready, 1)
                    v.tensor_scalar(rs2[:], rstd2[:], pow2[:, 4:5], None, ALU.mult)
                    link(v.scalar_tensor_tensor(out=nrm2[:], in0=moments[:, :, 0], scalar=-1.0, in1=rstd2[:],
                                                op0=ALU.mult, op1=ALU.mult))

                def add_projection(t):
                    wait(dve, b, proj_done, t + 1)
                    if t == 0:
                        wait(dve, b, res_ready, 1)
                    v.scalar_tensor_tensor(out=y_tmp[:, t], in0=slot["proj", t][:, 0:D], scalar=rs2[:, t:t + 1],
                                           in1=res[:, t], op0=ALU.mult, op1=ALU.add).then_inc(*sig(proj_added))
                    wait(dve, b, proj_added, t + 1)
                    v.scalar_tensor_tensor(out=y_ffn[:, t], in0=csum[:, 0], scalar=nrm2[:, t:t + 1],
                                           in1=y_tmp[:, t], op0=ALU.mult, op1=ALU.add).then_inc(*sig(ffn_ready))

                def scale_context(j):
                    wait(dve, b, pv_done, j + 1)
                    pv = slot["pv", j][:, 0:NP * VC].rearrange("p (u c) -> p u c", c=VC)
                    v.reciprocal(rden[:, j], pv[:, :, 2 * DH]).then_inc(*sig(rden_ready))
                    wait(dve, b, rden_ready, j + 1)
                    for a in range(2):
                        part = slice(a * W, (a + 1) * W)
                        last = v.tensor_tensor(ctxn[part, j], pv[part, :, a * DH:(a + 1) * DH],
                                               rden[part, j].unsqueeze(2).broadcast_to([W, NP, DH]), ALU.mult)
                    last.then_inc(*sig(ctx_ready))

                def context_lo(h):
                    wait(dve, b, ct_hi_ready, h + 1)
                    v.tensor_tensor(ct_lo[:].rearrange("p u (j q) -> p j u q", q=W)[:, h * HALF:(h + 1) * HALF],
                                    slot["ct", h][:].rearrange("p (j u q) -> p j u q", u=2, q=W),
                                    ct_hi[:].rearrange("p u (j q) -> p j u q", q=W)[:, h * HALF:(h + 1) * HALF],
                                    ALU.subtract).then_inc(*sig(ct_ready))

                def add_attention(t):
                    wait(dve, b, wo_done, t + 1)
                    if t == 0:
                        wait(dve, b, stored, 0)
                        wait(dve, b, ffn_ready, NT)
                    v.scalar_tensor_tensor(out=y_out[:, t], in0=slot["wo", t][:, 0:D], scalar=attn_scale[:, 0:1],
                                           in1=y_ffn[:, t], op0=ALU.mult, op1=ALU.add).then_inc(*sig(y_ready))

                for i in range(NF):
                    split_gelu(i)
                for j in range(4):
                    maximum(j)
                hidden_moments()
                split_maxima(0)
                maximum(4)
                maximum(5)
                hidden_scales()
                add_projection(0)
                add_projection(1)
                maximum(6)
                maximum(7)
                add_projection(2)
                split_maxima(1)
                add_projection(3)
                dve.wait_ge(PER[x_loaded][0], b * 16 + 32)
                statistics(link)
                scale_context(0)
                scale_context(1)
                dve.wait_ge(PER[rstd_ready][0], b + 2)
                wait(dve, b, xt_done, 1)
                normalize()
                for j in range(2, NJ):
                    scale_context(j)
                    if j == 5:
                        context_lo(0)
                context_lo(1)
                for t in range(NT):
                    add_attention(t)
                while n_step[0] < STEPS:
                    link(v.tensor_copy(msq[:, 0:1], rden[:, 0, 0:1]))

        @block.tensor
        def _(pe):
            mm = nc.tensor.matmul
            PARTS = ((0, 0), (0, 1), (1, 0))

            pe.wait_ge(consts_ready, 1)
            pe.wait_ge(proj_t_ready, 1)
            for c, vec in enumerate((lnw, lnb)):
                for i in range(NH):
                    last = mm(small[0][0:1, c * D:(c + 1) * D], vec[:, i:i + 1], proj_t32[:, i],
                              start=(i == 0), stop=(i == NH - 1))
            last.then_inc(crow_done, 1)
            pe.wait_ge(crow_ready, 1)
            mm(small[1][:], ones[0:1, :], crow[:], start=True, stop=True).then_inc(csum_done, 1)
            pe.wait_ge(csum_ready, 1)
            pe.wait_ge(weights_ready, 1)

            with pe.Fori(0, NB) as b:
                xt = (xt_hi, xt_lo)
                wt = (w_hi, w_lo)
                gt = (g_hi, g_lo)
                cts = (ct_hi, ct_lo)

                def job(kind, n):
                    ps = slot[kind, n]
                    wait_slot(pe, b, (kind, n))
                    if kind == "xt":
                        pe.wait_ge(PER[xn_ready][0], b + 1)
                        for k in range(KD):
                            for t in range(NT):
                                last = nc.tensor.transpose(ps[:, k, t * P:(t + 1) * P], xn[:, t, k * P:(k + 1) * P],
                                                           ident[:])
                        last.then_inc(*sig(xt_done))
                    elif kind == "qk":
                        if n == 0:
                            wait(pe, b, xt_ready, 1)
                        for m in range(KD):
                            i = 0
                            for k in range(KD):
                                for pw, px in PARTS:
                                    last = mm(ps[:, m], wt[pw][:, n, k, m * P:(m + 1) * P], xt[px][:, k],
                                              start=(i == 0), stop=(i == 3 * KD - 1))
                                    i += 1
                        last.then_inc(*sig(qk_done))
                    elif kind == "v":
                        for t in range(NT):
                            i = 0
                            for k in range(KD):
                                for px, pw in PARTS:
                                    last = mm(ps[:, t // 2, (t % 2) * D:(t % 2 + 1) * D],
                                              xt[px][:, k, t * P:(t + 1) * P], wt[pw][:, 2, k],
                                              start=(i == 0), stop=(i == 3 * KD - 1))
                                    i += 1
                        last.then_inc(*sig(v_done))
                    elif kind == "fc":
                        for a in range(2):
                            m = 2 * n + a
                            i = 0
                            for k in range(KD):
                                for px in range(2):
                                    last = mm(ps[:, a], fc_t[:, k, m * P:(m + 1) * P], xt[px][:, k],
                                              start=(i == 0), stop=(i == 2 * KD - 1))
                                    i += 1
                        last.then_inc(*sig(fc_done))
                    elif kind == "sa":
                        if n == 0:
                            wait(pe, b, stacks_loaded, 16)
                        for a in range(2):
                            mm(ps[:, a], onehot[:], mask_q[:, 1 if n == 0 else 0].rearrange("p u k -> p (u k)"),
                               start=True, stop=False)
                            for u in range(4):
                                i = a * 4 + u
                                last = mm(ps[:, a, u * P:(u + 1) * P],
                                          q_stack[:, i, n],
                                          k_stack[:, i, n * W:n * W + P], start=False, stop=(u == 3))
                        last.then_inc(*sig(sa_done))
                    elif kind == "mt":
                        wait(pe, b, max_ready, (n + 1) * HALF)
                        nc.tensor.transpose(ps[0:4 * NP, 0:P],
                                            negmax[:, n * HALF:(n + 1) * HALF].rearrange("p j u -> p (j u)"),
                                            ident[:]).then_inc(*sig(mt_done))
                    elif kind == "st":
                        if n % HALF == 0:
                            wait(pe, b, shift_loaded[n // HALF], 3)
                        for a in range(2):
                            mm(ps[:, a], mask_k[:, 1 if n == 0 else 0], shift[:, n, a * 512:(a + 1) * 512],
                               start=True, stop=False)
                            for u in range(4):
                                i = a * 4 + u
                                last = mm(ps[:, a, u * P:(u + 1) * P], k_stack[:, i, n * W:n * W + P],
                                          q_stack[:, i, n],
                                          start=False, stop=(u == 3))
                        last.then_inc(*sig(st_done))
                    elif kind == "mom":
                        wait(pe, b, sum_ready, SUMS)
                        for t in range(NT):
                            for c in range(2):
                                for a in range(2):
                                    last = mm(ps[:, 2 * t + c:2 * t + c + 1], gsum[:, c, a, t * P:(t + 1) * P],
                                              ones[:, 0:1], start=(a == 0), stop=(a == 1))
                        last.then_inc(*sig(mom_done))
                    elif kind == "proj":
                        if n == 0:
                            wait(pe, b, g_ready, NH)
                        for i in range(NH):
                            for pg in range(2):
                                last = mm(ps[:, 0:D], gt[pg][:, i, n * P:(n + 1) * P], proj_t[:, i],
                                          start=(i == 0 and pg == 0), stop=(i == NH - 1 and pg == 1))
                        last.then_inc(*sig(proj_done))
                    elif kind == "pv":
                        wait(pe, b, exp_ready, n + 1)
                        if n == 0:
                            wait(pe, b, v_shifted, 2)
                        vals = v_odd[:, n // 2] if n % 2 == 0 else v_even[:, n // 2]
                        for i in range(NP):
                            last = mm(ps[:, i * VC:(i + 1) * VC], probs[:, n % 3, i], vals[:, i],
                                      start=True, stop=True)
                        last.then_inc(*sig(pv_done))
                    elif kind == "ct":
                        wait(pe, b, ctx_ready, (n + 1) * HALF)
                        for i in range(HALF):
                            last = nc.tensor.transpose(ps[:, i * P:(i + 1) * P],
                                                       ctxn[:, n * HALF + i].rearrange("p u d -> p (u d)"), ident[:])
                        last.then_inc(*sig(ct_done))
                    elif kind == "wo":
                        wait(pe, b, ct_ready, n // 2 + 1)
                        i = 0
                        for u in range(2):
                            for pc, pw in PARTS:
                                last = mm(ps[:, 0:D], cts[pc][:, u, n * P:(n + 1) * P], wt[pw][:, 3, u],
                                          start=(i == 0), stop=(i == 5))
                                i += 1
                        last.then_inc(*sig(wo_done))

                for kind, n in ORDER:
                    job(kind, n)


_OUT_SHAPE = (8, 512, 256)


def kernel(**inputs):
    import numpy as _np
    import concourse.bacc as _bacc
    from concourse.bass_utils import run_bass_kernel_spmd as _run

    f = {k: _np.asarray(v) for k, v in inputs.items()}
    w_o = f["L0_attn_Wo"]

    def by_pair(w):
        return w.reshape(256, 8, 2, 16).transpose(0, 2, 3, 1).reshape(256, 256)

    laid = {
        "x": f["L0_attn_x"],
        "w_q": by_pair(f["L0_attn_Wq"]),
        "w_k": by_pair(f["L0_attn_Wk"]),
        "w_v": f["L0_attn_Wv"],
        "w_o": w_o.reshape(8, 2, 16, 256).transpose(1, 0, 2, 3).reshape(256, 256),
        "w_fc": f["L0_ffn_W_fc"].T,
        "ln_w": f["L0_ffn_ln_w"].reshape(8, 128).T,
        "ln_b": f["L0_ffn_ln_b"].reshape(8, 128).T,
        "w_proj": f["L0_ffn_W_proj"].T,
    }
    nc = _bacc.Bacc("TRN2", target_bir_lowering=False, num_devices=1)
    arrays, args = {}, []
    for name, a in laid.items():
        a = _np.ascontiguousarray(a)
        arrays[f"in_{name}"] = a
        args.append(nc.dram_tensor(f"in_{name}", a.shape, mybir.dt.from_np(a.dtype), kind="ExternalInput").ap())
    args.append(nc.dram_tensor("out_0", _OUT_SHAPE, mybir.dt.float32, kind="ExternalOutput").ap())
    attention_and_ternary_ffn(nc, *args)
    r = _run(nc, [arrays], core_ids=[0])
    return r.results[0]["out_0"]
```

```python
import concourse.bass as bass
from concourse import mybir
from contextlib import ExitStack


def attention_and_ternary_ffn(
    nc: bass.Bass,
    x: bass.AP,
    w_q: bass.AP,
    w_k: bass.AP,
    w_v: bass.AP,
    w_o: bass.AP,
    w_fc: bass.AP,
    ln_w: bass.AP,
    ln_b: bass.AP,
    w_proj: bass.AP,
    out: bass.AP,
):
    fp32 = mybir.dt.float32
    fp16 = mybir.dt.float16
    bf16 = mybir.dt.bfloat16
    u32 = mybir.dt.uint32
    ALU = mybir.AluOpType
    ACT = mybir.ActivationFunctionType
    AX = mybir.AxisListType

    P = 128
    NB, L, D = x.shape
    HID = w_fc.shape[1]
    H = 16
    DH = D // H
    W = 64
    NT = L // P
    KD = D // P
    NH = HID // P
    NF = NH // 2
    NJ = L // W
    NP = H // 2
    HALF = NJ // 2
    VC = 2 * DH + 1
    LN_EPS = 1e-5
    EPS = 1e-6
    NEG = -1e38
    SMALLEST = 2.0 ** -100

    ctx = ExitStack()
    with ctx:
        def sb(name, shape, dt):
            return ctx.enter_context(nc.sbuf_tensor(name, shape, dt))

        def sem(name):
            return ctx.enter_context(nc.semaphore(name))

        x_in = sb("x_in", [P, NT, D], fp32)
        w_hi = sb("w_hi", [P, 4, KD, D], fp16)
        w_lo = sb("w_lo", [P, 4, KD, D], fp16)
        fc_t = sb("fc_t", [P, KD, HID], fp16)
        proj_t = sb("proj_t", [P, NH, D], fp16)
        lnw = sb("lnw", [P, NH], fp32)
        lnb = sb("lnb", [P, NH], fp32)
        lnw_s = sb("lnw_s", [P, NH], fp32)
        red = sb("red", [P, 8], fp32)
        redall = sb("redall", [P, 8], fp32)
        scaled = sb("scaled", [P, 8], fp32)
        pow2 = sb("pow2", [P, 5], fp32)
        inv2 = sb("inv2", [P, 5], fp32)
        theta = sb("theta", [P, 2], fp32)
        ntheta = sb("ntheta", [P, 2], fp32)
        exp_scale = sb("exp_scale", [P, 1], fp32)
        attn_scale = sb("attn_scale", [P, 1], fp32)
        crow = sb("crow", [1, 2 * D], fp32)
        csum = sb("csum", [P, 2, D], fp32)
        ident = sb("ident", [P, P], fp32)
        ones = sb("ones", [P, P], fp32)
        expo = sb("expo", [P, NT], fp32)
        onehot = sb("onehot", [P, P], bf16)
        mask_q = sb("mask_q", [P, 2, 4, P], bf16)
        mask_k = sb("mask_k", [P, 2, P], bf16)
        bn6 = sb("bn6", [P, NT, 6], fp32)
        mv = sb("mv", [P, NT, 2], fp32)
        veps = sb("veps", [P, NT], fp32)
        rstd = sb("rstd", [P, NT], fp32)
        xn = sb("xn", [P, NT, D], fp32)
        res = sb("res", [P, NT, D], fp32)
        xt_hi = sb("xt_hi", [P, KD, L], fp16)
        xt_lo = sb("xt_lo", [P, KD, L], fp16)
        qk_split = sb("qk_split", [P, 2, KD, 2, L], fp16)
        q_stack = sb("q_stack", [P, NP, NJ, P], fp16)
        k_stack = sb("k_stack", [P, NP, W + L], fp16)
        v_even = sb("v_even", [P, 2, NT, NP, VC], fp16)
        v_odd = sb("v_odd", [P, 2, NT, NP, VC], fp16)
        gel = sb("gel", [P, NF, 2, L], fp32)
        gsq = sb("gsq", [P, NF, 2, L], fp32)
        fc_raw = gel[:, 0:NF // 2].rearrange("p i a n -> p (i a n)").rearrange("p (k n) -> p k n", k=KD)
        gsum = sb("gsum", [P, 2, 2, L], fp32)
        gsum2 = sb("gsum2", [P, 2, L], fp32)
        g_hi = sb("g_hi", [P, NH, L], fp16)
        g_lo = sb("g_lo", [P, NH, L], fp16)
        negmax = sb("negmax", [P, NJ, NP], fp32)
        mt = sb("mt", [4 * NP, 2, 3, P], bf16)
        mt_left = sb("mt_left", [4 * NP, 2, 2, P], fp32)
        shift = sb("shift", [P, NJ, NP * P], bf16)
        PB = 3
        probs = sb("probs", [P, PB, NP, P], fp32)
        p_parts = sb("p_parts", [P, 2, PB, NP, P], fp16)
        p_hi, p_lo = p_parts[:, 0], p_parts[:, 1]
        flat = p_parts[:].rearrange("p a s u n -> p (a s u n)")
        proj_t32 = flat[:, 0:2 * NH * D].bitcast(fp32).rearrange("p (k n) -> p k n", k=NH)
        below = flat[:, 2 * NH * D:3 * NH * D]
        w_raw = probs[:].rearrange("p s u n -> p (s u n)")[:, 0:4 * KD * D].rearrange("p (a k n) -> p a k n", a=4, k=KD)
        rden = sb("rden", [P, NJ, NP], fp32)
        ctxn = sb("ctxn", [P, NJ, NP, DH], fp32)
        ct_hi = sb("ct_hi", [P, 2, L], fp16)
        ct_lo = sb("ct_lo", [P, 2, L], fp16)
        moments = sb("moments", [P, NT, 2], fp32)
        msq = sb("msq", [P, NT], fp32)
        var2 = sb("var2", [P, NT], fp32)
        rstd2 = sb("rstd2", [P, NT], fp32)
        rs2 = sb("rs2", [P, NT], fp32)
        nrm2 = sb("nrm2", [P, NT], fp32)
        y_bufs = sb("y_bufs", [P, 3, NT, D], fp32)
        y_tmp, y_ffn, y_out = y_bufs[:, 0], y_bufs[:, 1], y_bufs[:, 2]
        proj_raw = y_bufs[:, 0:2].rearrange("p a t n -> p (a t) n")

        scratch = nc.dram_tensor("qk_scratch", [2, 2, D, L], fp16, kind="Internal").ap()

        big = [ctx.enter_context(nc.psum_tensor(f"big{i}", [P, 2, 512], fp32)) for i in range(3)]
        small = [ctx.enter_context(nc.psum_tensor(f"small{i}", [P, 512], fp32)) for i in range(2)]

        PER = {}

        def event(name, per, unit=1, ahead=0):
            PER[name] = (sem(name), per * unit, unit, per * unit if ahead else 0)
            return name

        x_loaded = event("x_loaded", 1, 16)
        scratch_written = [event(f"scratch_written{s}", 2, 16) for s in range(2)]
        stacks_loaded = event("stacks_loaded", 16, 16)
        v_shifted = event("v_shifted", 4, 16)
        shift_loaded = [event(f"shift_loaded{h}", 3, 16) for h in range(2)]
        stored = event("stored", NT, 16, ahead=1)
        xt_done = event("xt_done", 1)
        qk_done = event("qk_done", 2)
        v_done = event("v_done", 1)
        fc_done = event("fc_done", NF)
        sa_done = event("sa_done", NJ)
        mt_done = event("mt_done", 2)
        mom_done = event("mom_done", 1)
        proj_done = event("proj_done", NT)
        st_done = event("st_done", NJ)
        pv_done = event("pv_done", NJ)
        ct_done = event("ct_done", 2)
        wo_done = event("wo_done", NT)
        xt_hi_ready = event("xt_hi_ready", 1)
        qk_hi_ready = event("qk_hi_ready", 2)
        v_hi_ready = event("v_hi_ready", 1)
        gelu_ready = event("gelu_ready", NF)
        square_ready = event("square_ready", NF)
        exp_ready = event("exp_ready", NJ)
        p_hi_ready = event("p_hi_ready", NJ, ahead=1)
        ct_hi_ready = event("ct_hi_ready", 2)
        xn_ready = event("xn_ready", 1)
        veps_ready = event("veps_ready", 1)
        xt_ready = event("xt_ready", 1)
        qk_ready = event("qk_ready", 2)
        v_ready = event("v_ready", 1)
        g_hi_ready = event("g_hi_ready", NH)
        g_ready = event("g_ready", NH)
        max_ready = event("max_ready", NJ, ahead=1)
        mt_ready = event("mt_ready", 2, ahead=1)
        halves_ready = event("halves_ready", 1)
        moments_ready = event("moments_ready", 1, ahead=1)
        var_ready = event("var_ready", 1)
        proj_added = event("proj_added", NT, ahead=1)
        ffn_ready = event("ffn_ready", NT)
        rden_ready = event("rden_ready", NJ)
        ctx_ready = event("ctx_ready", NJ, ahead=1)
        ct_ready = event("ct_ready", 2, ahead=1)
        y_ready = event("y_ready", NT, ahead=1)
        ln_step = event("ln_step", 2)
        back_step = event("back_step", 9)
        res_ready = event("res_ready", 1)
        rstd_ready = event("rstd_ready", 1)
        rstd2_ready = event("rstd2_ready", 1)
        SUMS = 2 * (NF - 1)
        sum_ready = event("sum_ready", SUMS)
        ON_POOL = (2, 5)
        p_lo_pool = event("p_lo_pool", len(ON_POOL))
        p_lo_dve = event("p_lo_dve", NJ - len(ON_POOL))
        w_loaded = sem("w_loaded")
        fc_loaded = sem("fc_loaded")
        ln_loaded = sem("ln_loaded")
        pool_const = sem("pool_const")
        consts_ready = sem("consts_ready")
        dve_pre = sem("dve_pre")
        red_ready = sem("red_ready")
        red_done = sem("red_done")
        crow_done = sem("crow_done")
        crow_ready = sem("crow_ready")
        csum_done = sem("csum_done")
        weights_ready = sem("weights_ready")
        proj_t_ready = sem("proj_t_ready")
        csum_ready = sem("csum_ready")

        def count(b, name, n):
            _, per, unit, start = PER[name]
            return b * per + (n * unit + start)

        def wait(eng, b, name, n):
            eng.wait_ge(PER[name][0], count(b, name, n))

        def sig(name):
            return PER[name][0], PER[name][2]

        def start_ahead(eng, *names):
            for name in names:
                eng.sem_inc(PER[name][0], PER[name][3])

        FRONT = [("xt", 0), ("qk", 0), ("qk", 1), ("v", 0), ("fc", 0), ("fc", 1), ("fc", 2), ("fc", 3)]
        BOTH = [("sa", 0), ("sa", 1), ("sa", 2), ("mom", 0), ("sa", 3), ("xt", 0), ("sa", 4), ("mt", 0),
                ("proj", 0), ("sa", 5), ("sa", 6), ("proj", 1), ("sa", 7), ("qk", 0), ("mt", 1), ("st", 0),
                ("st", 1), ("proj", 2), ("st", 2), ("pv", 0), ("st", 3), ("pv", 1), ("qk", 1), ("st", 4),
                ("pv", 2), ("st", 5), ("pv", 3), ("proj", 3), ("st", 6), ("pv", 4), ("ct", 0), ("st", 7),
                ("pv", 5), ("pv", 6), ("pv", 7), ("v", 0), ("fc", 0), ("fc", 1), ("ct", 1), ("fc", 2),
                ("wo", 0), ("wo", 1), ("fc", 3), ("wo", 2), ("wo", 3)]
        BACK = [j for j in BOTH if j not in FRONT]
        READ_OUT = {"xt": xt_ready, "qk": qk_ready, "v": v_ready, "fc": gelu_ready, "sa": max_ready,
                    "mt": mt_ready, "mom": moments_ready, "proj": proj_added, "st": p_hi_ready,
                    "pv": ctx_ready, "ct": ct_ready, "wo": y_ready}
        IN_BIG = ("xt", "qk", "v", "fc", "sa", "st")
        slot = {}
        for ring, is_big in ((big, True), (small, False)):
            for i, j in enumerate([j for j in BOTH if (j[0] in IN_BIG) == is_big]):
                slot[j] = ring[i % len(ring)]

        def wait_slot(eng, b, order, i):
            mine = slot[order[i]]
            ahead = [j for j in order[:i] if slot[j] is mine]
            if ahead:
                kind, n = ahead[-1]
                wait(eng, b + 1 if (kind, n) in FRONT and order is not FRONT else b, READ_OUT[kind], n + 1)
            elif order is not FRONT:
                backs = [j for j in BOTH if slot[j] is mine and j not in FRONT]
                fronts = [j for j in BOTH if slot[j] is mine and j in FRONT]
                kind, n = backs[-1]
                assert PER[READ_OUT[kind]][3]
                wait(eng, b, READ_OUT[kind], n + 1 - PER[READ_OUT[kind]][1])
                if fronts:
                    kind, n = fronts[-1]
                    wait(eng, b, READ_OUT[kind], n + 1)

        block = ctx.enter_context(nc.Block())

        @block.sync
        def _(sp):
            def load_x(b):
                sp.dma_start(x_in[:], x[b].rearrange("(t p) d -> p t d", p=P)).then_inc(*sig(x_loaded))

            def write_scratch(b, s):
                for part, ready in enumerate((qk_hi_ready, qk_ready)):
                    wait(sp, b, ready, s + 1)
                    sp.dma_start(scratch[s, part].rearrange("(k p) n -> p k n", p=P),
                                 qk_split[:, s, :, part]).then_inc(*sig(scratch_written[s]))

            def load_stacks(b):
                for s in range(2):
                    wait(sp, b, scratch_written[s], 2)
                    for half in range(2):
                        for a in range(2):
                            for c in range(2):
                                r = half * 4 * DH + (a * 2 + c) * DH
                                src = scratch[s, a if s == 0 else c].rearrange("(u d i) n -> u d i n", u=2, d=DH)[half]
                                if s == 0:
                                    src = src.rearrange("d i (j q) -> d (i j) q", q=W)
                                    dst = q_stack[r:r + DH].rearrange("p i j (u q) -> p (i j) u q", u=2)[:, :, half]
                                else:
                                    dst = k_stack[r:r + DH, :, W:]
                                sp.dma_start(dst, src).then_inc(*sig(stacks_loaded))

            def shift_values(b):
                for part, ready in enumerate((v_hi_ready, v_ready)):
                    wait(sp, b, ready, 1)
                    sp.dma_start(v_odd[0:W, part, 1:NT], v_even[W:P, part, 0:NT - 1]).then_inc(*sig(v_shifted))
                    sp.dma_start(v_odd[W:P, part], v_even[0:W, part]).then_inc(*sig(v_shifted))

            def load_shift(b, h):
                wait(sp, b, mt_ready, h + 1)
                for c in range(3):
                    sp.dma_start(shift[W + c:W + c + 1, h * HALF:(h + 1) * HALF, :], mt[:, h, c, :]).then_inc(
                        *sig(shift_loaded[h]))

            def store(b):
                for t in range(NT):
                    wait(sp, b, y_ready, t + 1)
                    sp.dma_start(out[b, t * P:(t + 1) * P, :], y_out[:, t]).then_inc(*sig(stored))

            load_x(0)
            for i, w in enumerate((w_q, w_k, w_v, w_o)):
                sp.dma_start(w_raw[:, i], w.rearrange("(k p) n -> p k n", p=P)).then_inc(w_loaded, 16)
            sp.dma_start(lnw[:], ln_w).then_inc(ln_loaded, 16)
            sp.dma_start(lnb[:], ln_b).then_inc(ln_loaded, 16)
            sp.dma_start(fc_raw, w_fc.rearrange("(k p) n -> p k n", p=P)).then_inc(fc_loaded, 16)
            sp.dma_start(proj_raw, w_proj.rearrange("(k p) n -> p k n", p=P)).then_inc(fc_loaded, 16)
            sp.wait_ge(consts_ready, 1)
            start_ahead(sp, stored)
            for s in range(2):
                write_scratch(0, s)
            load_stacks(0)
            shift_values(0)
            wait(sp, 0, res_ready, 1)
            wait(sp, 0, xn_ready, 1)
            load_x(1)
            with sp.Fori(0, NB - 1) as b:
                nxt = (b + 2) % NB
                for v in [nxt * (L * D) * 4, b * (L * D) * 4, count(b, st_done, NJ)] + [
                        count(b, mt_ready, h + 1) for h in range(2)] + [
                        count(b, y_ready, t + 1) for t in range(NT)] + [
                        count(b + 1, name, n) for name, n in (
                            (qk_hi_ready, 1), (qk_hi_ready, 2), (qk_ready, 1), (qk_ready, 2), (res_ready, 1),
                            (scratch_written[0], 2), (v_hi_ready, 1), (v_ready, 1), (xn_ready, 1))]:
                    sp.compute_val(v)
                load_shift(b, 0)
                write_scratch(b + 1, 0)
                load_shift(b, 1)
                write_scratch(b + 1, 1)
                wait(sp, b + 1, xn_ready, 1)
                wait(sp, b + 1, res_ready, 1)
                load_x(nxt)
                wait(sp, b, st_done, NJ)
                load_stacks(b + 1)
                shift_values(b + 1)
                store(b)
            last = NB - 1
            load_shift(last, 0)
            load_shift(last, 1)
            store(last)
            wait(sp, last, stored, NT)

        @block.gpsimd
        def _(pool):
            g = nc.gpsimd
            steps = [0]

            def step(ins):
                steps[0] += 1
                ins.then_inc(pool_const, 1)
                pool.wait_ge(pool_const, steps[0])

            def token_rstd(b):
                wait(pool, b, veps_ready, 1)
                g.tensor_tensor(rstd[:], veps[:], expo[:], ALU.pow).then_inc(*sig(rstd_ready))

            def hidden_rstd(b):
                wait(pool, b, var_ready, 1)
                g.tensor_tensor(rstd2[:], var2[:], expo[:], ALU.pow).then_inc(*sig(rstd2_ready))

            def residual(b):
                wait(pool, b, x_loaded, 1)
                wait(pool, b, proj_added, 0)
                g.tensor_tensor(res[:], x_in[:], csum[:, 1:2, :].broadcast_to([P, NT, D]), ALU.add).then_inc(
                    *sig(res_ready))

            def hidden_sums(b):
                for i in range(1, NF):
                    for kind, src, ready in ((0, gel, gelu_ready), (1, gsq, square_ready)):
                        wait(pool, b, ready, i + 1)
                        if i > 1:
                            wait(pool, b, sum_ready, 2 * (i - 1) + kind - 1)
                        first = src[:, 0] if i == 1 else gsum[:, kind]
                        g.tensor_tensor(gsum[:, kind], first, src[:, i], ALU.add).then_inc(*sig(sum_ready))

            def lower_part(b, j):
                wait(pool, b, p_hi_ready, j + 1)
                g.tensor_tensor(p_lo[:, j % PB], probs[:, j % PB], p_hi[:, j % PB], ALU.subtract).then_inc(
                    *sig(p_lo_pool))

            step(g.memset(ident[:], 0.0))
            step(g.memset(expo[:], -0.5))
            step(g.affine_select(out=ident[:], in_=ident[:], compare_op=ALU.not_equal, fill=1.0, base=0,
                                 pattern=[[1, P]], channel_multiplier=-1))
            token_rstd(0)
            pool.wait_ge(red_ready, 1)
            g.partition_all_reduce(redall[:, 0:5], red[:, 0:5], P, bass.bass_isa.ReduceOp.max).then_inc(red_done, 1)
            pool.wait_ge(red_ready, 2)
            g.partition_all_reduce(redall[:, 5:7], red[:, 5:7], P, bass.bass_isa.ReduceOp.add).then_inc(red_done, 1)
            step(g.memset(ones[:], 1.0))
            step(g.memset(onehot[:], 0.0))
            step(g.memset(mask_q[:], 0.0))
            step(g.memset(mask_k[:], 0.0))
            oh = onehot[:].rearrange("p (a q) -> p a q", q=W)
            step(g.affine_select(out=oh, in_=oh, compare_op=ALU.not_equal, fill=1.0, base=0,
                                 pattern=[[0, 2], [1, W]], channel_multiplier=-1))
            for m in (mask_q[0:W].rearrange("p f u k -> p (f u) k"), mask_k[0:W]):
                n = m.shape[1]
                step(g.affine_select(out=m, in_=m, compare_op=ALU.is_gt, fill=NEG, base=0,
                                     pattern=[[0, n], [1, P]], channel_multiplier=-1))
                step(g.affine_select(out=m, in_=m, compare_op=ALU.is_ge, fill=NEG, base=W,
                                     pattern=[[0, n], [-1, P]], channel_multiplier=1))
            step(g.memset(mask_q[0:W, 1, :, 0:W], NEG))
            step(g.memset(mask_k[0:W, 1, 0:W], NEG))
            step(g.memset(mask_k[W:W + 3, :, :], 1.0))
            step(g.memset(shift[:].bitcast(u32), 0))
            sh = shift[:].rearrange("p j (u q) -> p (j u) q", q=W)
            step(g.affine_select(out=sh, in_=sh, compare_op=ALU.not_equal, fill=1.0, base=0,
                                 pattern=[[0, NJ * H], [1, W]], channel_multiplier=-1))
            step(g.memset(q_stack[:].bitcast(u32), 0))
            step(g.memset(k_stack[:, :, 0:W].bitcast(u32), 0))
            step(g.memset(v_odd[0:W, :, 0], 0.0))
            step(g.memset(v_even[:, 0, :, :, 2 * DH:], 1.0))
            g.memset(v_even[:, 1, :, :, 2 * DH:], 0.0).then_inc(consts_ready, 1)
            pool.wait_ge(csum_ready, 1)
            residual(0)
            hidden_sums(0)
            with pool.Fori(0, NB - 1) as b:
                for v in [count(b, name, n) for name, n in (
                        (var_ready, 1), (p_hi_ready, ON_POOL[0] + 1), (p_hi_ready, ON_POOL[1] + 1))] + [
                        count(b + 1, name, n) for name, n in (
                            (veps_ready, 1), (x_loaded, 1), (proj_added, 0), (gelu_ready, 2), (gelu_ready, 3),
                            (gelu_ready, 4), (sum_ready, 1), (sum_ready, 2), (sum_ready, 3), (sum_ready, 4))]:
                    pool.compute_val(v)
                token_rstd(b + 1)
                hidden_rstd(b)
                for j in ON_POOL:
                    lower_part(b, j)
                residual(b + 1)
                hidden_sums(b + 1)
            last = NB - 1
            hidden_rstd(last)
            for j in ON_POOL:
                lower_part(last, j)

        @block.scalar
        def _(act):
            s = nc.scalar

            def xt_upper(b):
                wait(act, b, xt_done, 1)
                s.activation(xt_hi[:], slot["xt", 0][:], ACT.Copy).then_inc(*sig(xt_hi_ready))

            def qk_upper(b, i):
                wait(act, b, qk_done, i + 1)
                s.activation(qk_split[:, i, :, 0, :], slot["qk", i][:], ACT.Copy).then_inc(*sig(qk_hi_ready))

            def v_upper(b):
                wait(act, b, v_done, 1)
                s.activation(v_even[:, 0, :, :, 0:2 * DH],
                             slot["v", 0][:].rearrange("p k (t i d) -> p (k t) i d", i=NP, d=2 * DH),
                             ACT.Copy).then_inc(*sig(v_hi_ready))

            def gelu(b, i):
                wait(act, b, fc_done, i + 1)
                s.activation(gel[:, i], slot["fc", i][:], ACT.Gelu).then_inc(*sig(gelu_ready))

            def square(b, i):
                wait(act, b, gelu_ready, i + 1)
                s.activation(gsq[:, i], gel[:, i], ACT.Square).then_inc(*sig(square_ready))

            def exp(b, j):
                wait(act, b, st_done, j + 1)
                if j >= PB:
                    wait(act, b, pv_done, j - PB + 1)
                st = slot["st", j][:].rearrange("p a (u n) -> p (a u) n", n=P)
                s.activation(probs[:, j % PB], st, ACT.Exp, scale=exp_scale[:, 0:1]).then_inc(*sig(exp_ready))
                s.activation(p_hi[:, j % PB], st, ACT.Exp, scale=exp_scale[:, 0:1]).then_inc(*sig(p_hi_ready))

            def context_upper(b, h):
                wait(act, b, ct_done, h + 1)
                s.activation(ct_hi[:].rearrange("p u (j q) -> p j u q", q=W)[:, h * HALF:(h + 1) * HALF],
                             slot["ct", h][:].rearrange("p (j u q) -> p j u q", u=2, q=W),
                             ACT.Copy).then_inc(*sig(ct_hi_ready))

            def both(b, front, back):
                f = b + 1
                if front:
                    xt_upper(f)
                    qk_upper(f, 0)
                for j in range(4):
                    exp(b, j)
                if front:
                    qk_upper(f, 1)
                for j in range(4, 7):
                    exp(b, j)
                context_upper(b, 0)
                exp(b, 7)
                if front:
                    v_upper(f)
                    gelu(f, 0)
                    gelu(f, 1)
                context_upper(b, 1)
                if front:
                    square(f, 0)
                    square(f, 1)
                    gelu(f, 2)
                    square(f, 2)
                    gelu(f, 3)
                    square(f, 3)

            start_ahead(act, p_hi_ready)
            xt_upper(0)
            qk_upper(0, 0)
            qk_upper(0, 1)
            v_upper(0)
            for i in range(NF):
                gelu(0, i)
                square(0, i)
            with act.Fori(0, NB - 1) as b:
                both(b, True, True)
            both(NB - 1, False, True)

        @block.vector
        def _(dve):
            v = nc.vector
            pre = [0]

            def link_pre(ins):
                pre[0] += 1
                ins.then_inc(dve_pre, 1)
                dve.wait_ge(dve_pre, pre[0])

            def link(ins, b, name, n):
                ins.then_inc(*sig(name))
                wait(dve, b, name, n)

            def statistics(b):
                wait(dve, b, x_loaded, 1)
                for t in range(NT):
                    last = v.bn_stats(bn6[:, t], x_in[:, t])
                link(last, b, ln_step, 1)
                v.memset(veps[:], 0.0)
                for t in range(NT):
                    last = v.bn_aggr(mv[:, t], bn6[:, t])
                link(last, b, ln_step, 2)
                v.tensor_scalar(veps[:], mv[:, :, 1], LN_EPS, None, ALU.add).then_inc(*sig(veps_ready))

            def normalize(b):
                wait(dve, b, rstd_ready, 1)
                for t in range(NT):
                    last = v.tensor_scalar(xn[:, t], x_in[:, t], mv[:, t, 0:1], rstd[:, t:t + 1],
                                           ALU.subtract, ALU.mult)
                last.then_inc(*sig(xn_ready))

            def xt_lower(b):
                wait(dve, b, xt_hi_ready, 1)
                v.tensor_tensor(xt_lo[:], slot["xt", 0][:], xt_hi[:], ALU.subtract).then_inc(*sig(xt_ready))

            def qk_lower(b, i):
                wait(dve, b, qk_hi_ready, i + 1)
                v.tensor_tensor(qk_split[:, i, :, 1, :], slot["qk", i][:], qk_split[:, i, :, 0, :],
                                ALU.subtract).then_inc(*sig(qk_ready))

            def v_lower(b):
                wait(dve, b, v_hi_ready, 1)
                v.tensor_tensor(v_even[:, 1, :, :, 0:2 * DH],
                                slot["v", 0][:].rearrange("p k (t i d) -> p (k t) i d", i=NP, d=2 * DH),
                                v_even[:, 0, :, :, 0:2 * DH], ALU.subtract).then_inc(*sig(v_ready))

            def split_gelu(b, i):
                wait(dve, b, gelu_ready, i + 1)
                for a in range(2):
                    v.tensor_scalar(g_hi[:, 2 * i + a], gel[:, i, a], lnw_s[:, 2 * i + a:2 * i + a + 1], None,
                                    ALU.mult).then_inc(*sig(g_hi_ready))
                for a in range(2):
                    wait(dve, b, g_hi_ready, 2 * i + a + 1)
                    v.scalar_tensor_tensor(out=g_lo[:, 2 * i + a], in0=gel[:, i, a],
                                           scalar=lnw_s[:, 2 * i + a:2 * i + a + 1], in1=g_hi[:, 2 * i + a],
                                           op0=ALU.mult, op1=ALU.subtract).then_inc(*sig(g_ready))

            def maximum(b, j):
                wait(dve, b, sa_done, j + 1)
                v.tensor_reduce(negmax[:, j], slot["sa", j][:].rearrange("p a (u k) -> p (a u) k", k=P),
                                AX.X, ALU.max, negate=True).then_inc(*sig(max_ready))

            def split_maxima(b, h):
                wait(dve, b, mt_done, h + 1)
                row = slot["mt", h][0:4 * NP, 0:P]
                link(v.tensor_copy(mt[:, h, 0], row), b, back_step, 3 * (1 + h) + 1)
                link(v.tensor_tensor(mt_left[:, h, 0], row, mt[:, h, 0], ALU.subtract), b, back_step, 3 * (1 + h) + 2)
                link(v.tensor_copy(mt[:, h, 1], mt_left[:, h, 0]), b, back_step, 3 * (1 + h) + 3)
                v.tensor_tensor(mt[:, h, 2], mt_left[:, h, 0], mt[:, h, 1], ALU.subtract).then_inc(*sig(mt_ready))

            def add_halves(b):
                wait(dve, b, sum_ready, SUMS)
                v.tensor_tensor(gsum2[:], gsum[:, :, 0], gsum[:, :, 1], ALU.add).then_inc(*sig(halves_ready))

            def hidden_moments(b):
                wait(dve, b, mom_done, 1)
                v.tensor_scalar(moments[:], slot["mom", 0][:, 0:2 * NT].rearrange("p (t a) -> p t a", a=2),
                                1.0 / HID, None, ALU.mult).then_inc(*sig(moments_ready))
                wait(dve, b, moments_ready, 1)
                link(v.tensor_tensor(msq[:], moments[:, :, 0], moments[:, :, 0], ALU.mult), b, back_step, 1)
                link(v.tensor_tensor(var2[:], moments[:, :, 1], msq[:], ALU.subtract), b, back_step, 2)
                v.tensor_scalar(var2[:], var2[:], 0.0, LN_EPS, ALU.max, ALU.add).then_inc(*sig(var_ready))

            def hidden_scales(b):
                wait(dve, b, rstd2_ready, 1)
                v.tensor_scalar(rs2[:], rstd2[:], pow2[:, 4:5], None, ALU.mult)
                link(v.scalar_tensor_tensor(out=nrm2[:], in0=moments[:, :, 0], scalar=-1.0, in1=rstd2[:],
                                            op0=ALU.mult, op1=ALU.mult), b, back_step, 3)

            def add_projection(b, t):
                wait(dve, b, proj_done, t + 1)
                if t == 0:
                    wait(dve, b, res_ready, 1)
                v.scalar_tensor_tensor(out=y_tmp[:, t], in0=slot["proj", t][:, 0:D], scalar=rs2[:, t:t + 1],
                                       in1=res[:, t], op0=ALU.mult, op1=ALU.add).then_inc(*sig(proj_added))
                wait(dve, b, proj_added, t + 1)
                v.scalar_tensor_tensor(out=y_ffn[:, t], in0=csum[:, 0], scalar=nrm2[:, t:t + 1],
                                       in1=y_tmp[:, t], op0=ALU.mult, op1=ALU.add).then_inc(*sig(ffn_ready))

            def lower_part(b, j):
                if j not in ON_POOL:
                    wait(dve, b, p_hi_ready, j + 1)
                    v.tensor_tensor(p_lo[:, j % PB], probs[:, j % PB], p_hi[:, j % PB], ALU.subtract).then_inc(
                        *sig(p_lo_dve))

            def scale_context(b, j):
                wait(dve, b, pv_done, j + 1)
                pv = slot["pv", j][:, 0:NP * VC].rearrange("p (u c) -> p u c", c=VC)
                v.reciprocal(rden[:, j], pv[:, :, 2 * DH]).then_inc(*sig(rden_ready))
                wait(dve, b, rden_ready, j + 1)
                for a in range(2):
                    part = slice(a * W, (a + 1) * W)
                    last = v.tensor_tensor(ctxn[part, j], pv[part, :, a * DH:(a + 1) * DH],
                                           rden[part, j].unsqueeze(2).broadcast_to([W, NP, DH]), ALU.mult)
                last.then_inc(*sig(ctx_ready))

            def context_lower(b, h):
                wait(dve, b, ct_hi_ready, h + 1)
                v.tensor_tensor(ct_lo[:].rearrange("p u (j q) -> p j u q", q=W)[:, h * HALF:(h + 1) * HALF],
                                slot["ct", h][:].rearrange("p (j u q) -> p j u q", u=2, q=W),
                                ct_hi[:].rearrange("p u (j q) -> p j u q", q=W)[:, h * HALF:(h + 1) * HALF],
                                ALU.subtract).then_inc(*sig(ct_ready))

            def add_attention(b, t):
                wait(dve, b, wo_done, t + 1)
                if t == 0:
                    wait(dve, b, stored, 0)
                    wait(dve, b, ffn_ready, NT)
                v.scalar_tensor_tensor(out=y_out[:, t], in0=slot["wo", t][:, 0:D], scalar=attn_scale[:, 0:1],
                                       in1=y_ffn[:, t], op0=ALU.mult, op1=ALU.add).then_inc(*sig(y_ready))

            def both(b, front):
                f = b + 1
                if front:
                    statistics(f)
                maximum(b, 0)
                maximum(b, 1)
                add_halves(b)
                maximum(b, 2)
                if front:
                    wait(dve, b, xt_done, 1)
                    normalize(f)
                hidden_moments(b)
                maximum(b, 3)
                if front:
                    xt_lower(f)
                maximum(b, 4)
                hidden_scales(b)
                split_maxima(b, 0)
                add_projection(b, 0)
                maximum(b, 5)
                maximum(b, 6)
                add_projection(b, 1)
                maximum(b, 7)
                if front:
                    qk_lower(f, 0)
                split_maxima(b, 1)
                lower_part(b, 0)
                add_projection(b, 2)
                lower_part(b, 1)
                scale_context(b, 0)
                lower_part(b, 2)
                scale_context(b, 1)
                lower_part(b, 3)
                if front:
                    qk_lower(f, 1)
                scale_context(b, 2)
                lower_part(b, 4)
                scale_context(b, 3)
                add_projection(b, 3)
                lower_part(b, 5)
                scale_context(b, 4)
                lower_part(b, 6)
                context_lower(b, 0)
                scale_context(b, 5)
                lower_part(b, 7)
                scale_context(b, 6)
                scale_context(b, 7)
                if front:
                    v_lower(f)
                    split_gelu(f, 0)
                context_lower(b, 1)
                if front:
                    split_gelu(f, 1)
                add_attention(b, 0)
                add_attention(b, 1)
                if front:
                    split_gelu(f, 2)
                add_attention(b, 2)
                add_attention(b, 3)
                if front:
                    split_gelu(f, 3)

            start_ahead(dve, max_ready, mt_ready, moments_ready, proj_added, ctx_ready, ct_ready, y_ready)
            statistics(0)
            dve.wait_ge(w_loaded, 64)
            v.tensor_reduce(red[:, 0:4], w_raw.rearrange("p a k n -> p a (k n)"), AX.X, ALU.max,
                            apply_absolute_value=True)
            dve.wait_ge(ln_loaded, 32)
            v.tensor_reduce(red[:, 4:5], lnw[:], AX.X, ALU.max, apply_absolute_value=True).then_inc(red_ready, 1)
            normalize(0)
            dve.wait_ge(fc_loaded, 32)
            v.tensor_reduce(red[:, 5:6], fc_raw.rearrange("p k n -> p (k n)"), AX.X, ALU.add,
                            apply_absolute_value=True)
            v.tensor_reduce(red[:, 6:7], proj_raw.rearrange("p k n -> p (k n)"), AX.X, ALU.add,
                            apply_absolute_value=True).then_inc(red_ready, 1)
            dve.wait_ge(red_done, 1)
            link_pre(v.tensor_scalar(scaled[:, 0:5], redall[:, 0:5], SMALLEST, None, ALU.max))
            link_pre(v.tensor_scalar(pow2[:].bitcast(u32), scaled[:, 0:5].bitcast(u32), 0x7F800000, None,
                                     ALU.bitwise_and))
            link_pre(v.reciprocal(inv2[:], pow2[:]))
            v.tensor_scalar(exp_scale[:], pow2[:, 0:1], pow2[:, 1:2], DH ** -0.5, ALU.mult, ALU.mult)
            v.tensor_scalar(attn_scale[:], pow2[:, 2:3], pow2[:, 3:4], None, ALU.mult)
            v.tensor_scalar(lnw_s[:], lnw[:], inv2[:, 4:5], None, ALU.mult)
            for i in range(4):
                last = v.tensor_scalar(w_hi[:, i], w_raw[:, i], inv2[:, i:i + 1], None, ALU.mult)
            link_pre(last)
            for i in range(4):
                last = v.scalar_tensor_tensor(out=w_lo[:, i], in0=w_raw[:, i], scalar=inv2[:, i:i + 1],
                                              in1=w_hi[:, i], op0=ALU.mult, op1=ALU.subtract)
            last.then_inc(weights_ready, 1)
            xt_lower(0)
            dve.wait_ge(red_done, 2)
            link_pre(v.tensor_scalar(scaled[:, 5:7], redall[:, 5:7], 1.0 / (D * HID), EPS, ALU.mult, ALU.add))
            v.tensor_scalar(theta[:], scaled[:, 5:7], 0.5, None, ALU.mult)
            link_pre(v.tensor_scalar(ntheta[:], scaled[:, 5:7], -0.5, None, ALU.mult))
            bl = below.rearrange("p (k n) -> p k n", k=KD)
            link_pre(v.tensor_scalar(bl, fc_raw, ntheta[:, 0:1], None, ALU.is_lt))
            v.scalar_tensor_tensor(out=fc_t[:], in0=fc_raw, scalar=theta[:, 0:1], in1=bl,
                                   op0=ALU.is_gt, op1=ALU.subtract).then_inc(weights_ready, 1)
            qk_lower(0, 0)
            qk_lower(0, 1)
            dve.wait_ge(weights_ready, 2)
            bl = below.rearrange("p (k n) -> p k n", k=NH)
            link_pre(v.tensor_scalar(bl, proj_raw, ntheta[:, 1:2], None, ALU.is_lt))
            v.scalar_tensor_tensor(out=proj_t32, in0=proj_raw, scalar=theta[:, 1:2], in1=bl,
                                   op0=ALU.is_gt, op1=ALU.subtract).then_inc(proj_t_ready, 1)
            dve.wait_ge(proj_t_ready, 1)
            v.tensor_copy(proj_t[:], proj_t32).then_inc(weights_ready, 1)
            v_lower(0)
            dve.wait_ge(crow_done, 1)
            v.tensor_copy(crow[:], small[0][0:1, :]).then_inc(crow_ready, 1)
            dve.wait_ge(csum_done, 1)
            v.tensor_copy(csum[:].rearrange("p a n -> p (a n)"), small[1][:]).then_inc(csum_ready, 1)
            for i in range(NF):
                split_gelu(0, i)
            with dve.Fori(0, NB - 1) as b:
                both(b, True)
            both(NB - 1, False)

        @block.tensor
        def _(pe):
            mm = nc.tensor.matmul
            PARTS = ((0, 0), (0, 1), (1, 0))
            xt = (xt_hi, xt_lo)
            wt = (w_hi, w_lo)
            gt = (g_hi, g_lo)
            cts = (ct_hi, ct_lo)
            ps_hl = (p_hi, p_lo)

            def job(b, kind, n):
                ps = slot[kind, n]
                if kind == "xt":
                    wait(pe, b, xn_ready, 1)
                    for k in range(KD):
                        for t in range(NT):
                            last = nc.tensor.transpose(ps[:, k, t * P:(t + 1) * P], xn[:, t, k * P:(k + 1) * P],
                                                       ident[:])
                    last.then_inc(*sig(xt_done))
                elif kind == "qk":
                    if n == 0:
                        wait(pe, b, xt_ready, 1)
                    for m in range(KD):
                        i = 0
                        for k in range(KD):
                            for pw, px in PARTS:
                                last = mm(ps[:, m], wt[pw][:, n, k, m * P:(m + 1) * P], xt[px][:, k],
                                          start=(i == 0), stop=(i == 3 * KD - 1))
                                i += 1
                    last.then_inc(*sig(qk_done))
                elif kind == "v":
                    for t in range(NT):
                        i = 0
                        for k in range(KD):
                            for px, pw in PARTS:
                                last = mm(ps[:, t // 2, (t % 2) * D:(t % 2 + 1) * D],
                                          xt[px][:, k, t * P:(t + 1) * P], wt[pw][:, 2, k],
                                          start=(i == 0), stop=(i == 3 * KD - 1))
                                i += 1
                    last.then_inc(*sig(v_done))
                elif kind == "fc":
                    for a in range(2):
                        m = 2 * n + a
                        i = 0
                        for k in range(KD):
                            for px in range(2):
                                last = mm(ps[:, a], fc_t[:, k, m * P:(m + 1) * P], xt[px][:, k],
                                          start=(i == 0), stop=(i == 2 * KD - 1))
                                i += 1
                    last.then_inc(*sig(fc_done))
                elif kind == "sa":
                    if n == 0:
                        wait(pe, b, stacks_loaded, 16)
                    for a in range(2):
                        mm(ps[:, a], onehot[:], mask_q[:, 1 if n == 0 else 0].rearrange("p u k -> p (u k)"),
                           start=True, stop=False)
                        for u in range(4):
                            i = a * 4 + u
                            last = mm(ps[:, a, u * P:(u + 1) * P], q_stack[:, i, n],
                                      k_stack[:, i, n * W:n * W + P], start=False, stop=(u == 3))
                    last.then_inc(*sig(sa_done))
                elif kind == "mt":
                    wait(pe, b, max_ready, (n + 1) * HALF)
                    nc.tensor.transpose(ps[0:4 * NP, 0:P],
                                        negmax[:, n * HALF:(n + 1) * HALF].rearrange("p j u -> p (j u)"),
                                        ident[:]).then_inc(*sig(mt_done))
                elif kind == "st":
                    if n % HALF == 0:
                        wait(pe, b, shift_loaded[n // HALF], 3)
                    for a in range(2):
                        mm(ps[:, a], mask_k[:, 1 if n == 0 else 0], shift[:, n, a * 512:(a + 1) * 512],
                           start=True, stop=False)
                        for u in range(4):
                            i = a * 4 + u
                            last = mm(ps[:, a, u * P:(u + 1) * P], k_stack[:, i, n * W:n * W + P],
                                      q_stack[:, i, n], start=False, stop=(u == 3))
                    last.then_inc(*sig(st_done))
                elif kind == "mom":
                    wait(pe, b, halves_ready, 1)
                    for t in range(NT):
                        for c in range(2):
                            last = mm(ps[:, 2 * t + c:2 * t + c + 1], gsum2[:, c, t * P:(t + 1) * P],
                                      ones[:, 0:1], start=True, stop=True)
                    last.then_inc(*sig(mom_done))
                elif kind == "proj":
                    if n == 0:
                        wait(pe, b, g_ready, NH)
                    for i in range(NH):
                        for pg in range(2):
                            last = mm(ps[:, 0:D], gt[pg][:, i, n * P:(n + 1) * P], proj_t[:, i],
                                      start=(i == 0 and pg == 0), stop=(i == NH - 1 and pg == 1))
                    last.then_inc(*sig(proj_done))
                elif kind == "pv":
                    if n in ON_POOL:
                        wait(pe, b, p_lo_pool, ON_POOL.index(n) + 1)
                    else:
                        wait(pe, b, p_lo_dve, n + 1 - sum(j < n for j in ON_POOL))
                    if n == 0:
                        wait(pe, b, v_shifted, 4)
                    vals = v_odd if n % 2 == 0 else v_even
                    for i in range(NP):
                        for k, (pp, pw) in enumerate(PARTS):
                            last = mm(ps[:, i * VC:(i + 1) * VC], ps_hl[pp][:, n % PB, i], vals[:, pw, n // 2, i],
                                      start=(k == 0), stop=(k == 2))
                    last.then_inc(*sig(pv_done))
                elif kind == "ct":
                    wait(pe, b, ctx_ready, (n + 1) * HALF)
                    for i in range(HALF):
                        last = nc.tensor.transpose(ps[:, i * P:(i + 1) * P],
                                                   ctxn[:, n * HALF + i].rearrange("p u d -> p (u d)"), ident[:])
                    last.then_inc(*sig(ct_done))
                elif kind == "wo":
                    wait(pe, b, ct_ready, n // 2 + 1)
                    i = 0
                    for u in range(2):
                        for pc, pw in PARTS:
                            last = mm(ps[:, 0:D], cts[pc][:, u, n * P:(n + 1) * P], wt[pw][:, 3, u],
                                      start=(i == 0), stop=(i == 5))
                            i += 1
                    last.then_inc(*sig(wo_done))

            def run(b, order):
                for i, (kind, n) in enumerate(order):
                    wait_slot(pe, b, order, i)
                    job(b + 1 if (kind, n) in FRONT and order is not FRONT else b, kind, n)

            pe.wait_ge(pool_const, 3)
            for i, (kind, n) in enumerate(FRONT):
                if kind == "qk" and n == 0:
                    pe.wait_ge(weights_ready, 1)
                if kind == "fc" and n == 0:
                    pe.wait_ge(weights_ready, 2)
                wait_slot(pe, 0, FRONT, i)
                job(0, kind, n)
            pe.wait_ge(consts_ready, 1)
            pe.wait_ge(proj_t_ready, 1)
            for c, vec in enumerate((lnw, lnb)):
                for i in range(NH):
                    last = mm(small[0][0:1, c * D:(c + 1) * D], vec[:, i:i + 1], proj_t32[:, i],
                              start=(i == 0), stop=(i == NH - 1))
            last.then_inc(crow_done, 1)
            pe.wait_ge(crow_ready, 1)
            mm(small[1][:], ones[0:1, :], crow[:], start=True, stop=True).then_inc(csum_done, 1)
            pe.wait_ge(csum_ready, 1)
            pe.wait_ge(weights_ready, 3)
            with pe.Fori(0, NB - 1) as b:
                run(b, BOTH)
            run(NB - 1, BACK)


_OUT_SHAPE = (8, 512, 256)


def kernel(**inputs):
    import numpy as _np
    import concourse.bacc as _bacc
    from concourse.bass_utils import run_bass_kernel_spmd as _run

    f = {k: _np.asarray(v) for k, v in inputs.items()}
    w_o = f["L0_attn_Wo"]

    def by_pair(w):
        return w.reshape(256, 8, 2, 16).transpose(0, 2, 3, 1).reshape(256, 256)

    laid = {
        "x": f["L0_attn_x"],
        "w_q": by_pair(f["L0_attn_Wq"]),
        "w_k": by_pair(f["L0_attn_Wk"]),
        "w_v": f["L0_attn_Wv"],
        "w_o": w_o.reshape(8, 2, 16, 256).transpose(1, 0, 2, 3).reshape(256, 256),
        "w_fc": f["L0_ffn_W_fc"].T,
        "ln_w": f["L0_ffn_ln_w"].reshape(8, 128).T,
        "ln_b": f["L0_ffn_ln_b"].reshape(8, 128).T,
        "w_proj": f["L0_ffn_W_proj"].T,
    }
    nc = _bacc.Bacc("TRN2", target_bir_lowering=False, num_devices=1)
    arrays, args = {}, []
    for name, a in laid.items():
        a = _np.ascontiguousarray(a)
        arrays[f"in_{name}"] = a
        args.append(nc.dram_tensor(f"in_{name}", a.shape, mybir.dt.from_np(a.dtype), kind="ExternalInput").ap())
    args.append(nc.dram_tensor("out_0", _OUT_SHAPE, mybir.dt.float32, kind="ExternalOutput").ap())
    attention_and_ternary_ffn(nc, *args)
    r = _run(nc, [arrays], core_ids=[0])
    return r.results[0]["out_0"]
```

```python
import concourse.bass as bass
from concourse import mybir
from contextlib import ExitStack


def attention_and_ternary_ffn(
    nc: bass.Bass,
    x: bass.AP,
    w_q: bass.AP,
    w_k: bass.AP,
    w_v: bass.AP,
    w_o: bass.AP,
    w_fc: bass.AP,
    ln_w: bass.AP,
    ln_b: bass.AP,
    w_proj: bass.AP,
    out: bass.AP,
):
    fp32 = mybir.dt.float32
    fp16 = mybir.dt.float16
    bf16 = mybir.dt.bfloat16
    u32 = mybir.dt.uint32
    ALU = mybir.AluOpType
    ACT = mybir.ActivationFunctionType
    AX = mybir.AxisListType

    P = 128
    NB, L, D = x.shape
    HID = w_fc.shape[1]
    H = 16
    DH = D // H
    W = 64
    NT = L // P
    KD = D // P
    NH = HID // P
    NF = NH // 2
    NJ = L // W
    NP = H // 2
    HALF = NJ // 2
    VC = 2 * DH + 1
    LN_EPS = 1e-5
    EPS = 1e-6
    NEG = -1e38
    SMALLEST = 2.0 ** -100

    ctx = ExitStack()
    with ctx:
        def sb(name, shape, dt):
            return ctx.enter_context(nc.sbuf_tensor(name, shape, dt))

        def sem(name):
            return ctx.enter_context(nc.semaphore(name))

        x_in = sb("x_in", [P, NT, D], fp32)
        w_hi = sb("w_hi", [P, 4, KD, D], fp16)
        w_lo = sb("w_lo", [P, 4, KD, D], fp16)
        fc_t = sb("fc_t", [P, KD, HID], fp16)
        proj_t = sb("proj_t", [P, NH, D], fp16)
        lnw = sb("lnw", [P, NH], fp32)
        lnb = sb("lnb", [P, NH], fp32)
        lnw_s = sb("lnw_s", [P, NH], fp32)
        red = sb("red", [P, 8], fp32)
        redall = sb("redall", [P, 8], fp32)
        scaled = sb("scaled", [P, 8], fp32)
        pow2 = sb("pow2", [P, 5], fp32)
        inv2 = sb("inv2", [P, 5], fp32)
        theta = sb("theta", [P, 2], fp32)
        ntheta = sb("ntheta", [P, 2], fp32)
        exp_scale = sb("exp_scale", [P, 1], fp32)
        attn_scale = sb("attn_scale", [P, 1], fp32)
        crow = sb("crow", [1, 2 * D], fp32)
        csum = sb("csum", [P, 2, D], fp32)
        ident = sb("ident", [P, P], fp32)
        ones = sb("ones", [P, P], fp32)
        expo = sb("expo", [P, NT], fp32)
        onehot = sb("onehot", [P, P], bf16)
        mask_q = sb("mask_q", [P, 2, 4, P], bf16)
        mask_k = sb("mask_k", [P, 2, P], bf16)
        bn6 = sb("bn6", [P, NT, 6], fp32)
        mv = sb("mv", [P, NT, 2], fp32)
        veps = sb("veps", [P, NT], fp32)
        rstd = sb("rstd", [P, NT], fp32)
        xn = sb("xn", [P, NT, D], fp32)
        res = sb("res", [P, NT, D], fp32)
        xt_hi = sb("xt_hi", [P, KD, L], fp16)
        xt_lo = sb("xt_lo", [P, KD, L], fp16)
        qk_split = sb("qk_split", [P, 2, KD, 2, L], fp16)
        q_stack = sb("q_stack", [P, NP, NJ, P], fp16)
        k_stack = sb("k_stack", [P, NP, W + L], fp16)
        v_even = sb("v_even", [P, 2, NT, NP, VC], fp16)
        v_odd = sb("v_odd", [P, 2, NT, NP, VC], fp16)
        gel = sb("gel", [P, NF, 2, L], fp32)
        gsq = sb("gsq", [P, NF, 2, L], fp32)
        fc_raw = gel[:, 0:NF // 2].rearrange("p i a n -> p (i a n)").rearrange("p (k n) -> p k n", k=KD)
        gsum = sb("gsum", [P, 2, 2, L], fp32)
        gsum2 = sb("gsum2", [P, 2, L], fp32)
        g_hi = sb("g_hi", [P, NH, L], fp16)
        g_lo = sb("g_lo", [P, NH, L], fp16)
        negmax = sb("negmax", [P, NJ, NP], fp32)
        mt = sb("mt", [4 * NP, 2, 3, P], bf16)
        mt_left = sb("mt_left", [4 * NP, 2, 2, P], fp32)
        shift = sb("shift", [P, NJ, NP * P], bf16)
        PB = 3
        probs = sb("probs", [P, PB, NP, P], fp32)
        p_parts = sb("p_parts", [P, 2, PB, NP, P], fp16)
        p_hi, p_lo = p_parts[:, 0], p_parts[:, 1]
        flat = p_parts[:].rearrange("p a s u n -> p (a s u n)")
        proj_t32 = flat[:, 0:2 * NH * D].bitcast(fp32).rearrange("p (k n) -> p k n", k=NH)
        below = flat[:, 2 * NH * D:3 * NH * D]
        w_raw = probs[:].rearrange("p s u n -> p (s u n)")[:, 0:4 * KD * D].rearrange("p (a k n) -> p a k n", a=4, k=KD)
        rden = sb("rden", [P, NJ, NP], fp32)
        ctxn = sb("ctxn", [P, NJ, NP, DH], fp32)
        ct_hi = sb("ct_hi", [P, 2, L], fp16)
        ct_lo = sb("ct_lo", [P, 2, L], fp16)
        moments = sb("moments", [P, NT, 2], fp32)
        msq = sb("msq", [P, NT], fp32)
        var2 = sb("var2", [P, NT], fp32)
        rstd2 = sb("rstd2", [P, NT], fp32)
        rs2 = sb("rs2", [P, NT], fp32)
        nrm2 = sb("nrm2", [P, NT], fp32)
        y_bufs = sb("y_bufs", [P, 3, NT, D], fp32)
        y_tmp, y_ffn, y_out = y_bufs[:, 0], y_bufs[:, 1], y_bufs[:, 2]
        proj_raw = y_bufs[:, 0:2].rearrange("p a t n -> p (a t) n")

        scratch = nc.dram_tensor("qk_scratch", [2, 2, D, L], fp16, kind="Internal").ap()

        big = [ctx.enter_context(nc.psum_tensor(f"big{i}", [P, 2, 512], fp32)) for i in range(3)]
        small = [ctx.enter_context(nc.psum_tensor(f"small{i}", [P, 512], fp32)) for i in range(2)]

        PER = {}

        def event(name, per, unit=1, ahead=0):
            PER[name] = (sem(name), per * unit, unit, per * unit if ahead else 0)
            return name

        x_loaded = event("x_loaded", 1, 16)
        scratch_written = [event(f"scratch_written{s}", 2, 16) for s in range(2)]
        stacks_loaded = event("stacks_loaded", 16, 16)
        v_shifted = event("v_shifted", 4, 16)
        shift_loaded = [event(f"shift_loaded{h}", 3, 16) for h in range(2)]
        stored = event("stored", NT, 16, ahead=1)
        xt_done = event("xt_done", 1)
        qk_done = event("qk_done", 2)
        v_done = event("v_done", 1)
        fc_done = event("fc_done", NF)
        sa_done = event("sa_done", NJ)
        mt_done = event("mt_done", 2)
        mom_done = event("mom_done", 1)
        proj_done = event("proj_done", NT)
        st_done = event("st_done", NJ)
        pv_done = event("pv_done", NJ)
        ct_done = event("ct_done", 2)
        wo_done = event("wo_done", NT)
        xt_hi_ready = event("xt_hi_ready", 1)
        qk_hi_ready = event("qk_hi_ready", 2)
        v_hi_ready = event("v_hi_ready", 1)
        gelu_ready = event("gelu_ready", NF)
        square_ready = event("square_ready", NF)
        exp_ready = event("exp_ready", NJ)
        p_hi_ready = event("p_hi_ready", NJ, ahead=1)
        ct_hi_ready = event("ct_hi_ready", 2)
        xn_ready = event("xn_ready", 1)
        veps_ready = event("veps_ready", 1)
        xt_ready = event("xt_ready", 1)
        qk_ready = event("qk_ready", 2)
        v_ready = event("v_ready", 1)
        g_hi_ready = event("g_hi_ready", NH)
        g_ready = event("g_ready", NH)
        max_ready = event("max_ready", NJ, ahead=1)
        mt_ready = event("mt_ready", 2, ahead=1)
        halves_ready = event("halves_ready", 1)
        moments_ready = event("moments_ready", 1, ahead=1)
        var_ready = event("var_ready", 1)
        proj_added = event("proj_added", NT, ahead=1)
        ffn_ready = event("ffn_ready", NT)
        rden_ready = event("rden_ready", NJ)
        ctx_ready = event("ctx_ready", NJ, ahead=1)
        ct_ready = event("ct_ready", 2, ahead=1)
        y_ready = event("y_ready", NT, ahead=1)
        ln_step = event("ln_step", 2)
        moment_step = event("moment_step", 3)
        max_step = event("max_step", 6)
        res_ready = event("res_ready", 1)
        rstd_ready = event("rstd_ready", 1)
        rstd2_ready = event("rstd2_ready", 1)
        SUMS = 2 * (NF - 1)
        sum_ready = event("sum_ready", SUMS)
        ON_POOL = (5,)
        p_lo_pool = event("p_lo_pool", len(ON_POOL))
        p_lo_dve = event("p_lo_dve", NJ - len(ON_POOL))
        w_loaded = sem("w_loaded")
        fc_loaded = sem("fc_loaded")
        ln_loaded = sem("ln_loaded")
        pool_const = sem("pool_const")
        consts_ready = sem("consts_ready")
        dve_pre = sem("dve_pre")
        red_ready = sem("red_ready")
        red_done = sem("red_done")
        crow_done = sem("crow_done")
        crow_ready = sem("crow_ready")
        csum_done = sem("csum_done")
        onehot_ready = sem("onehot_ready")
        tiles_zeroed = sem("tiles_zeroed")
        shift_filled = sem("shift_filled")
        scales_ready = sem("scales_ready")
        w_hi_ready = sem("w_hi_ready")
        w_ready = sem("w_ready")
        ternary_ready = sem("ternary_ready")
        proj_t_ready = sem("proj_t_ready")
        csum_ready = sem("csum_ready")

        def count(b, name, n):
            _, per, unit, start = PER[name]
            return b * per + (n * unit + start)

        def wait(eng, b, name, n):
            eng.wait_ge(PER[name][0], count(b, name, n))

        def sig(name):
            return PER[name][0], PER[name][2]

        def start_ahead(eng, *names):
            for name in names:
                eng.sem_inc(PER[name][0], PER[name][3])

        FRONT = [("xt", 0), ("qk", 0), ("qk", 1), ("v", 0), ("fc", 0), ("fc", 1), ("fc", 2), ("fc", 3)]
        BOTH = [("sa", 0), ("sa", 1), ("sa", 2), ("sa", 3), ("sa", 4), ("mom", 0), ("mt", 0), ("sa", 5), ("sa", 6), ("sa", 7),
                ("proj", 0), ("proj", 1), ("xt", 0), ("st", 0), ("st", 1), ("proj", 2), ("st", 2), ("mt", 1), ("qk", 0),
                ("pv", 0), ("st", 3), ("qk", 1), ("st", 4), ("pv", 1), ("st", 5), ("pv", 2), ("st", 6), ("pv", 3), ("st", 7),
                ("pv", 4), ("proj", 3), ("fc", 0), ("pv", 5), ("ct", 0), ("fc", 1), ("pv", 6), ("fc", 2), ("pv", 7), ("wo", 0),
                ("fc", 3), ("wo", 1), ("ct", 1), ("v", 0), ("wo", 2), ("wo", 3)]
        BACK = [j for j in BOTH if j not in FRONT]
        READ_OUT = {"xt": xt_ready, "qk": qk_ready, "v": v_ready, "fc": gelu_ready, "sa": max_ready,
                    "mt": mt_ready, "mom": moments_ready, "proj": proj_added, "st": p_hi_ready,
                    "pv": ctx_ready, "ct": ct_ready, "wo": y_ready}
        IN_BIG = ("xt", "qk", "v", "fc", "sa", "st")
        slot = {}
        for ring, is_big in ((big, True), (small, False)):
            for i, j in enumerate([j for j in BOTH if (j[0] in IN_BIG) == is_big]):
                slot[j] = ring[i % len(ring)]

        def wait_slot(eng, b, order, i):
            mine = slot[order[i]]
            ahead = [j for j in order[:i] if slot[j] is mine]
            if ahead:
                kind, n = ahead[-1]
                wait(eng, b + 1 if (kind, n) in FRONT and order is not FRONT else b, READ_OUT[kind], n + 1)
            elif order is not FRONT:
                backs = [j for j in BOTH if slot[j] is mine and j not in FRONT]
                fronts = [j for j in BOTH if slot[j] is mine and j in FRONT]
                kind, n = backs[-1]
                assert PER[READ_OUT[kind]][3]
                wait(eng, b, READ_OUT[kind], n + 1 - PER[READ_OUT[kind]][1])
                for kind, n in fronts:
                    wait(eng, b, READ_OUT[kind], n + 1)

        block = ctx.enter_context(nc.Block())

        @block.sync
        def _(sp):
            def load_x(b):
                sp.dma_start(x_in[:], x[b].rearrange("(t p) d -> p t d", p=P)).then_inc(*sig(x_loaded))

            def write_scratch(b, s):
                for part, ready in enumerate((qk_hi_ready, qk_ready)):
                    wait(sp, b, ready, s + 1)
                    sp.dma_start(scratch[s, part].rearrange("(k p) n -> p k n", p=P),
                                 qk_split[:, s, :, part]).then_inc(*sig(scratch_written[s]))

            def load_stack(b, s):
                wait(sp, b, scratch_written[s], 2)
                for half in range(2):
                    for a in range(2):
                        for c in range(2):
                            r = half * 4 * DH + (a * 2 + c) * DH
                            src = scratch[s, a if s == 0 else c].rearrange("(u d i) n -> u d i n", u=2, d=DH)[half]
                            if s == 0:
                                src = src.rearrange("d i (j q) -> d (i j) q", q=W)
                                dst = q_stack[r:r + DH].rearrange("p i j (u q) -> p (i j) u q", u=2)[:, :, half]
                            else:
                                dst = k_stack[r:r + DH, :, W:]
                            sp.dma_start(dst, src).then_inc(*sig(stacks_loaded))

            def shift_values(b):
                for part, ready in enumerate((v_hi_ready, v_ready)):
                    wait(sp, b, ready, 1)
                    sp.dma_start(v_odd[0:W, part, 1:NT], v_even[W:P, part, 0:NT - 1]).then_inc(*sig(v_shifted))
                    sp.dma_start(v_odd[W:P, part], v_even[0:W, part]).then_inc(*sig(v_shifted))

            def load_shift(b, h):
                wait(sp, b, mt_ready, h + 1)
                for c in range(3):
                    sp.dma_start(shift[W + c:W + c + 1, h * HALF:(h + 1) * HALF, :], mt[:, h, c, :]).then_inc(
                        *sig(shift_loaded[h]))

            def store(b, t):
                wait(sp, b, y_ready, t + 1)
                sp.dma_start(out[b, t * P:(t + 1) * P, :], y_out[:, t]).then_inc(*sig(stored))

            load_x(0)
            for i, w in enumerate((w_q, w_k, w_v, w_o)):
                sp.dma_start(w_raw[:, i], w.rearrange("(k p) n -> p k n", p=P)).then_inc(w_loaded, 16)
            sp.dma_start(lnw[:], ln_w).then_inc(ln_loaded, 16)
            sp.dma_start(lnb[:], ln_b).then_inc(ln_loaded, 16)
            sp.dma_start(fc_raw, w_fc.rearrange("(k p) n -> p k n", p=P)).then_inc(fc_loaded, 16)
            sp.dma_start(proj_raw, w_proj.rearrange("(k p) n -> p k n", p=P)).then_inc(fc_loaded, 16)
            start_ahead(sp, stored)
            for s in range(2):
                write_scratch(0, s)
            sp.wait_ge(tiles_zeroed, 1)
            for s in range(2):
                load_stack(0, s)
            shift_values(0)
            wait(sp, 0, res_ready, 1)
            wait(sp, 0, xn_ready, 1)
            load_x(1)
            sp.wait_ge(shift_filled, 1)
            with sp.Fori(0, NB - 1) as b:
                nxt = (b + 2) % NB
                for v in [nxt * (L * D) * 4, b * (L * D) * 4, count(b, st_done, NJ)] + [
                        count(b, mt_ready, h + 1) for h in range(2)] + [
                        count(b, y_ready, t + 1) for t in range(NT)] + [
                        count(b + 1, name, n) for name, n in (
                            (qk_hi_ready, 1), (qk_hi_ready, 2), (qk_ready, 1), (qk_ready, 2), (res_ready, 1),
                            (scratch_written[0], 2), (v_hi_ready, 1), (v_ready, 1), (xn_ready, 1))]:
                    sp.compute_val(v)
                load_shift(b, 0)
                load_shift(b, 1)
                write_scratch(b + 1, 0)
                write_scratch(b + 1, 1)
                wait(sp, b, st_done, NJ)
                load_stack(b + 1, 0)
                load_stack(b + 1, 1)
                wait(sp, b + 1, xn_ready, 1)
                wait(sp, b + 1, res_ready, 1)
                load_x(nxt)
                shift_values(b + 1)
                store(b, 0)
                store(b, 1)
                store(b, 2)
                store(b, 3)
            last = NB - 1
            load_shift(last, 0)
            load_shift(last, 1)
            for t in range(NT):
                store(last, t)
            wait(sp, last, stored, NT)

        @block.gpsimd
        def _(pool):
            g = nc.gpsimd
            steps = [0]

            def step(ins):
                steps[0] += 1
                ins.then_inc(pool_const, 1)
                pool.wait_ge(pool_const, steps[0])

            def token_rstd(b):
                wait(pool, b, veps_ready, 1)
                g.tensor_tensor(rstd[:], veps[:], expo[:], ALU.pow).then_inc(*sig(rstd_ready))

            def hidden_rstd(b):
                wait(pool, b, var_ready, 1)
                g.tensor_tensor(rstd2[:], var2[:], expo[:], ALU.pow).then_inc(*sig(rstd2_ready))

            def residual(b):
                wait(pool, b, x_loaded, 1)
                wait(pool, b, proj_added, 0)
                g.tensor_tensor(res[:], x_in[:], csum[:, 1:2, :].broadcast_to([P, NT, D]), ALU.add).then_inc(
                    *sig(res_ready))

            def hidden_sum(b, n):
                i, kind = n // 2 + 1, n % 2
                src, ready = ((gel, gelu_ready), (gsq, square_ready))[kind]
                wait(pool, b, ready, i + 1)
                if i > 1:
                    wait(pool, b, sum_ready, n - 1)
                first = src[:, 0] if i == 1 else gsum[:, kind]
                g.tensor_tensor(gsum[:, kind], first, src[:, i], ALU.add).then_inc(*sig(sum_ready))

            def lower_part(b, j):
                wait(pool, b, p_hi_ready, j + 1)
                g.tensor_tensor(p_lo[:, j % PB], probs[:, j % PB], p_hi[:, j % PB], ALU.subtract).then_inc(
                    *sig(p_lo_pool))

            step(g.memset(ident[:], 0.0))
            step(g.memset(expo[:], -0.5))
            step(g.affine_select(out=ident[:], in_=ident[:], compare_op=ALU.not_equal, fill=1.0, base=0,
                                 pattern=[[1, P]], channel_multiplier=-1))
            step(g.memset(onehot[:], 0.0))
            oh = onehot[:].rearrange("p (a q) -> p a q", q=W)
            g.affine_select(out=oh, in_=oh, compare_op=ALU.not_equal, fill=1.0, base=0,
                            pattern=[[0, 2], [1, W]], channel_multiplier=-1).then_inc(onehot_ready, 1)
            pool.wait_ge(onehot_ready, 1)
            step(g.memset(q_stack[:].bitcast(u32), 0))
            step(g.memset(k_stack[:, :, 0:W].bitcast(u32), 0))
            token_rstd(0)
            step(g.memset(v_odd[0:W, :, 0], 0.0))
            step(g.memset(v_even[:, 0, :, :, 2 * DH:], 1.0))
            g.memset(v_even[:, 1, :, :, 2 * DH:], 0.0).then_inc(tiles_zeroed, 1)
            pool.wait_ge(tiles_zeroed, 1)
            pool.wait_ge(red_ready, 1)
            g.partition_all_reduce(redall[:, 0:5], red[:, 0:5], P, bass.bass_isa.ReduceOp.max).then_inc(red_done, 1)
            step(g.memset(ones[:], 1.0))
            step(g.memset(mask_q[:], 0.0))
            step(g.memset(mask_k[:], 0.0))
            for m in (mask_q[0:W].rearrange("p f u k -> p (f u) k"), mask_k[0:W]):
                n = m.shape[1]
                step(g.affine_select(out=m, in_=m, compare_op=ALU.is_gt, fill=NEG, base=0,
                                     pattern=[[0, n], [1, P]], channel_multiplier=-1))
                step(g.affine_select(out=m, in_=m, compare_op=ALU.is_ge, fill=NEG, base=W,
                                     pattern=[[0, n], [-1, P]], channel_multiplier=1))
            step(g.memset(mask_q[0:W, 1, :, 0:W], NEG))
            step(g.memset(mask_k[0:W, 1, 0:W], NEG))
            g.memset(mask_k[W:W + 3, :, :], 1.0).then_inc(consts_ready, 1)
            pool.wait_ge(consts_ready, 1)
            pool.wait_ge(red_ready, 2)
            g.partition_all_reduce(redall[:, 5:7], red[:, 5:7], P, bass.bass_isa.ReduceOp.add).then_inc(red_done, 1)
            for n in range(SUMS):
                hidden_sum(0, n)
            pool.wait_ge(csum_ready, 1)
            residual(0)
            with pool.Fori(0, NB - 1) as b:
                for v in [count(b, name, n) for name, n in (
                        (var_ready, 1), (halves_ready, 1), *((p_hi_ready, j + 1) for j in ON_POOL))] + [
                        count(b + 1, name, n) for name, n in (
                            (veps_ready, 1), (x_loaded, 1), (proj_added, 0), (gelu_ready, 2), (gelu_ready, 3),
                            (gelu_ready, 4), (sum_ready, 1), (sum_ready, 2), (sum_ready, 3), (sum_ready, 4))]:
                    pool.compute_val(v)
                hidden_rstd(b)
                token_rstd(b + 1)
                lower_part(b, 5)
                wait(pool, b, halves_ready, 1)
                hidden_sum(b + 1, 0)
                hidden_sum(b + 1, 1)
                hidden_sum(b + 1, 2)
                hidden_sum(b + 1, 3)
                hidden_sum(b + 1, 4)
                hidden_sum(b + 1, 5)
                residual(b + 1)
            last = NB - 1
            hidden_rstd(last)
            for j in ON_POOL:
                lower_part(last, j)

        @block.scalar
        def _(act):
            s = nc.scalar

            def xt_upper(b):
                wait(act, b, xt_done, 1)
                s.activation(xt_hi[:], slot["xt", 0][:], ACT.Copy).then_inc(*sig(xt_hi_ready))

            def qk_upper(b, i):
                wait(act, b, qk_done, i + 1)
                s.activation(qk_split[:, i, :, 0, :], slot["qk", i][:], ACT.Copy).then_inc(*sig(qk_hi_ready))

            def v_upper(b):
                wait(act, b, v_done, 1)
                s.activation(v_even[:, 0, :, :, 0:2 * DH],
                             slot["v", 0][:].rearrange("p k (t i d) -> p (k t) i d", i=NP, d=2 * DH),
                             ACT.Copy).then_inc(*sig(v_hi_ready))

            def gelu(b, i):
                wait(act, b, fc_done, i + 1)
                s.activation(gel[:, i], slot["fc", i][:], ACT.Gelu).then_inc(*sig(gelu_ready))

            def square(b, i):
                wait(act, b, gelu_ready, i + 1)
                s.activation(gsq[:, i], gel[:, i], ACT.Square).then_inc(*sig(square_ready))

            def exp(b, j):
                wait(act, b, st_done, j + 1)
                if j >= PB:
                    wait(act, b, pv_done, j - PB + 1)
                st = slot["st", j][:].rearrange("p a (u n) -> p (a u) n", n=P)
                s.activation(probs[:, j % PB], st, ACT.Exp, scale=exp_scale[:, 0:1]).then_inc(*sig(exp_ready))
                s.activation(p_hi[:, j % PB], st, ACT.Exp, scale=exp_scale[:, 0:1]).then_inc(*sig(p_hi_ready))

            def context_upper(b, h):
                wait(act, b, ct_done, h + 1)
                s.activation(ct_hi[:].rearrange("p u (j q) -> p j u q", q=W)[:, h * HALF:(h + 1) * HALF],
                             slot["ct", h][:].rearrange("p (j u q) -> p j u q", u=2, q=W),
                             ACT.Copy).then_inc(*sig(ct_hi_ready))

            def gelu_upper(b, i):
                wait(act, b, gelu_ready, i + 1)
                for a in range(2):
                    s.activation(g_hi[:, 2 * i + a], gel[:, i, a], ACT.Copy,
                                 scale=lnw_s[:, 2 * i + a:2 * i + a + 1]).then_inc(*sig(g_hi_ready))

            def both(b, front):
                f = b + 1
                if front:
                    xt_upper(f)
                exp(b, 0)
                exp(b, 1)
                exp(b, 2)
                if front:
                    qk_upper(f, 0)
                exp(b, 3)
                if front:
                    qk_upper(f, 1)
                exp(b, 4)
                exp(b, 5)
                exp(b, 6)
                exp(b, 7)
                if front:
                    wait(act, b, g_ready, NH)
                    wait(act, b, sum_ready, SUMS)
                    gelu(f, 0)
                context_upper(b, 0)
                if front:
                    gelu(f, 1)
                    wait(act, b, proj_done, NT)
                    gelu_upper(f, 0)
                    square(f, 0)
                    square(f, 1)
                    gelu(f, 2)
                    gelu_upper(f, 1)
                    gelu_upper(f, 2)
                    square(f, 2)
                    gelu(f, 3)
                context_upper(b, 1)
                if front:
                    gelu_upper(f, 3)
                    wait(act, b, pv_done, NJ)
                    v_upper(f)
                    square(f, 3)

            start_ahead(act, p_hi_ready)
            act.wait_ge(onehot_ready, 1)
            s.activation(shift[:].rearrange("p j (u q) -> p (j u) q", q=W),
                         onehot[:, 0:W].unsqueeze(1).broadcast_to([P, NJ * H, W]), ACT.Copy).then_inc(shift_filled, 1)
            act.wait_ge(scales_ready, 1)
            for i in range(2):
                s.activation(w_hi[:, i], w_raw[:, i], ACT.Copy, scale=inv2[:, i:i + 1]).then_inc(w_hi_ready, 1)
            xt_upper(0)
            for i in range(2, 4):
                s.activation(w_hi[:, i], w_raw[:, i], ACT.Copy, scale=inv2[:, i:i + 1]).then_inc(w_hi_ready, 1)
            qk_upper(0, 0)
            qk_upper(0, 1)
            v_upper(0)
            for i in range(NF):
                gelu(0, i)
                square(0, i)
            act.wait_ge(w_ready, 1)
            for i in range(NF):
                gelu_upper(0, i)
            with act.Fori(0, NB - 1) as b:
                both(b, True)
            both(NB - 1, False)

        @block.vector
        def _(dve):
            v = nc.vector
            pre = [0]

            def link_pre(ins):
                pre[0] += 1
                ins.then_inc(dve_pre, 1)
                dve.wait_ge(dve_pre, pre[0])

            def link(ins, b, name, n):
                ins.then_inc(*sig(name))
                wait(dve, b, name, n)

            def statistics(b):
                wait(dve, b, x_loaded, 1)
                for t in range(NT):
                    last = v.bn_stats(bn6[:, t], x_in[:, t])
                link(last, b, ln_step, 1)
                v.memset(veps[:], 0.0)
                for t in range(NT):
                    last = v.bn_aggr(mv[:, t], bn6[:, t])
                link(last, b, ln_step, 2)
                v.tensor_scalar(veps[:], mv[:, :, 1], LN_EPS, None, ALU.add).then_inc(*sig(veps_ready))

            def normalize(b):
                wait(dve, b, rstd_ready, 1)
                for t in range(NT):
                    last = v.tensor_scalar(xn[:, t], x_in[:, t], mv[:, t, 0:1], rstd[:, t:t + 1],
                                           ALU.subtract, ALU.mult)
                last.then_inc(*sig(xn_ready))

            def xt_lower(b):
                wait(dve, b, xt_hi_ready, 1)
                v.tensor_tensor(xt_lo[:], slot["xt", 0][:], xt_hi[:], ALU.subtract).then_inc(*sig(xt_ready))

            def qk_lower(b, i):
                wait(dve, b, qk_hi_ready, i + 1)
                v.tensor_tensor(qk_split[:, i, :, 1, :], slot["qk", i][:], qk_split[:, i, :, 0, :],
                                ALU.subtract).then_inc(*sig(qk_ready))

            def v_lower(b):
                wait(dve, b, v_hi_ready, 1)
                v.tensor_tensor(v_even[:, 1, :, :, 0:2 * DH],
                                slot["v", 0][:].rearrange("p k (t i d) -> p (k t) i d", i=NP, d=2 * DH),
                                v_even[:, 0, :, :, 0:2 * DH], ALU.subtract).then_inc(*sig(v_ready))

            def gelu_lower(b, i):
                wait(dve, b, g_hi_ready, 2 * i + 2)
                for a in range(2):
                    v.scalar_tensor_tensor(out=g_lo[:, 2 * i + a], in0=gel[:, i, a],
                                           scalar=lnw_s[:, 2 * i + a:2 * i + a + 1], in1=g_hi[:, 2 * i + a],
                                           op0=ALU.mult, op1=ALU.subtract).then_inc(*sig(g_ready))

            def maximum(b, j):
                wait(dve, b, sa_done, j + 1)
                v.tensor_reduce(negmax[:, j], slot["sa", j][:].rearrange("p a (u k) -> p (a u) k", k=P),
                                AX.X, ALU.max, negate=True).then_inc(*sig(max_ready))

            def split_maxima(b, h):
                wait(dve, b, mt_done, h + 1)
                row = slot["mt", h][0:4 * NP, 0:P]
                link(v.tensor_copy(mt[:, h, 0], row), b, max_step, 3 * h + 1)
                link(v.tensor_tensor(mt_left[:, h, 0], row, mt[:, h, 0], ALU.subtract), b, max_step, 3 * h + 2)
                link(v.tensor_copy(mt[:, h, 1], mt_left[:, h, 0]), b, max_step, 3 * h + 3)
                v.tensor_tensor(mt[:, h, 2], mt_left[:, h, 0], mt[:, h, 1], ALU.subtract).then_inc(*sig(mt_ready))

            def add_halves(b):
                wait(dve, b, sum_ready, SUMS)
                v.tensor_tensor(gsum2[:], gsum[:, :, 0], gsum[:, :, 1], ALU.add).then_inc(*sig(halves_ready))

            def hidden_moments(b):
                wait(dve, b, mom_done, 1)
                v.tensor_scalar(moments[:], slot["mom", 0][:, 0:2 * NT].rearrange("p (t a) -> p t a", a=2),
                                1.0 / HID, None, ALU.mult).then_inc(*sig(moments_ready))
                wait(dve, b, moments_ready, 1)
                link(v.tensor_tensor(msq[:], moments[:, :, 0], moments[:, :, 0], ALU.mult), b, moment_step, 1)
                link(v.tensor_tensor(var2[:], moments[:, :, 1], msq[:], ALU.subtract), b, moment_step, 2)
                v.tensor_scalar(var2[:], var2[:], 0.0, LN_EPS, ALU.max, ALU.add).then_inc(*sig(var_ready))

            def hidden_scales(b):
                wait(dve, b, rstd2_ready, 1)
                v.tensor_scalar(rs2[:], rstd2[:], pow2[:, 4:5], None, ALU.mult)
                link(v.scalar_tensor_tensor(out=nrm2[:], in0=moments[:, :, 0], scalar=-1.0, in1=rstd2[:],
                                            op0=ALU.mult, op1=ALU.mult), b, moment_step, 3)

            def add_projection(b, t):
                wait(dve, b, proj_done, t + 1)
                if t == 0:
                    wait(dve, b, res_ready, 1)
                v.scalar_tensor_tensor(out=y_tmp[:, t], in0=slot["proj", t][:, 0:D], scalar=rs2[:, t:t + 1],
                                       in1=res[:, t], op0=ALU.mult, op1=ALU.add).then_inc(*sig(proj_added))
                wait(dve, b, proj_added, t + 1)
                v.scalar_tensor_tensor(out=y_ffn[:, t], in0=csum[:, 0], scalar=nrm2[:, t:t + 1],
                                       in1=y_tmp[:, t], op0=ALU.mult, op1=ALU.add).then_inc(*sig(ffn_ready))

            def lower_part(b, j):
                if j not in ON_POOL:
                    wait(dve, b, p_hi_ready, j + 1)
                    v.tensor_tensor(p_lo[:, j % PB], probs[:, j % PB], p_hi[:, j % PB], ALU.subtract).then_inc(
                        *sig(p_lo_dve))

            def scale_context(b, j):
                wait(dve, b, pv_done, j + 1)
                pv = slot["pv", j][:, 0:NP * VC].rearrange("p (u c) -> p u c", c=VC)
                v.reciprocal(rden[:, j], pv[:, :, 2 * DH]).then_inc(*sig(rden_ready))
                wait(dve, b, rden_ready, j + 1)
                for a in range(2):
                    part = slice(a * W, (a + 1) * W)
                    last = v.tensor_tensor(ctxn[part, j], pv[part, :, a * DH:(a + 1) * DH],
                                           rden[part, j].unsqueeze(2).broadcast_to([W, NP, DH]), ALU.mult)
                last.then_inc(*sig(ctx_ready))

            def context_lower(b, h):
                wait(dve, b, ct_hi_ready, h + 1)
                v.tensor_tensor(ct_lo[:].rearrange("p u (j q) -> p j u q", q=W)[:, h * HALF:(h + 1) * HALF],
                                slot["ct", h][:].rearrange("p (j u q) -> p j u q", u=2, q=W),
                                ct_hi[:].rearrange("p u (j q) -> p j u q", q=W)[:, h * HALF:(h + 1) * HALF],
                                ALU.subtract).then_inc(*sig(ct_ready))

            def add_attention(b, t):
                wait(dve, b, wo_done, t + 1)
                if t == 0:
                    wait(dve, b, stored, 0)
                    wait(dve, b, ffn_ready, NT)
                v.scalar_tensor_tensor(out=y_out[:, t], in0=slot["wo", t][:, 0:D], scalar=attn_scale[:, 0:1],
                                       in1=y_ffn[:, t], op0=ALU.mult, op1=ALU.add).then_inc(*sig(y_ready))

            def both(b, front):
                f = b + 1
                maximum(b, 0)
                maximum(b, 1)
                add_halves(b)
                maximum(b, 2)
                maximum(b, 3)
                maximum(b, 4)
                hidden_moments(b)
                split_maxima(b, 0)
                if front:
                    statistics(f)
                maximum(b, 5)
                if front:
                    wait(dve, b, xt_done, 1)
                    normalize(f)
                maximum(b, 6)
                hidden_scales(b)
                maximum(b, 7)
                add_projection(b, 0)
                if front:
                    xt_lower(f)
                add_projection(b, 1)
                add_projection(b, 2)
                split_maxima(b, 1)
                lower_part(b, 0)
                lower_part(b, 1)
                lower_part(b, 2)
                if front:
                    qk_lower(f, 0)
                scale_context(b, 0)
                lower_part(b, 3)
                if front:
                    qk_lower(f, 1)
                scale_context(b, 1)
                scale_context(b, 2)
                lower_part(b, 4)
                scale_context(b, 3)
                scale_context(b, 4)
                add_projection(b, 3)
                scale_context(b, 5)
                lower_part(b, 6)
                lower_part(b, 7)
                context_lower(b, 0)
                scale_context(b, 6)
                if front:
                    gelu_lower(f, 0)
                scale_context(b, 7)
                add_attention(b, 0)
                if front:
                    gelu_lower(f, 1)
                    gelu_lower(f, 2)
                add_attention(b, 1)
                context_lower(b, 1)
                if front:
                    gelu_lower(f, 3)
                add_attention(b, 2)
                if front:
                    v_lower(f)
                add_attention(b, 3)

            start_ahead(dve, max_ready, mt_ready, moments_ready, proj_added, ctx_ready, ct_ready, y_ready)
            statistics(0)
            dve.wait_ge(w_loaded, 64)
            v.tensor_reduce(red[:, 0:4], w_raw.rearrange("p a k n -> p a (k n)"), AX.X, ALU.max,
                            apply_absolute_value=True)
            dve.wait_ge(ln_loaded, 32)
            v.tensor_reduce(red[:, 4:5], lnw[:], AX.X, ALU.max, apply_absolute_value=True).then_inc(red_ready, 1)
            normalize(0)
            dve.wait_ge(red_done, 1)
            link_pre(v.tensor_scalar(scaled[:, 0:5], redall[:, 0:5], SMALLEST, None, ALU.max))
            link_pre(v.tensor_scalar(pow2[:].bitcast(u32), scaled[:, 0:5].bitcast(u32), 0x7F800000, None,
                                     ALU.bitwise_and))
            v.reciprocal(inv2[:], pow2[:]).then_inc(scales_ready, 1)
            dve.wait_ge(scales_ready, 1)
            v.tensor_scalar(exp_scale[:], pow2[:, 0:1], pow2[:, 1:2], DH ** -0.5, ALU.mult, ALU.mult)
            v.tensor_scalar(attn_scale[:], pow2[:, 2:3], pow2[:, 3:4], None, ALU.mult)
            v.tensor_scalar(lnw_s[:], lnw[:], inv2[:, 4:5], None, ALU.mult)

            def weight_lower(i):
                dve.wait_ge(w_hi_ready, i + 1)
                v.scalar_tensor_tensor(out=w_lo[:, i], in0=w_raw[:, i], scalar=inv2[:, i:i + 1],
                                       in1=w_hi[:, i], op0=ALU.mult, op1=ALU.subtract).then_inc(w_ready, 1)

            weight_lower(0)
            weight_lower(1)
            xt_lower(0)
            dve.wait_ge(fc_loaded, 32)
            v.tensor_reduce(red[:, 5:6], fc_raw.rearrange("p k n -> p (k n)"), AX.X, ALU.add,
                            apply_absolute_value=True)
            v.tensor_reduce(red[:, 6:7], proj_raw.rearrange("p k n -> p (k n)"), AX.X, ALU.add,
                            apply_absolute_value=True).then_inc(red_ready, 1)
            qk_lower(0, 0)
            weight_lower(2)
            weight_lower(3)
            dve.wait_ge(red_done, 2)
            link_pre(v.tensor_scalar(scaled[:, 5:7], redall[:, 5:7], 1.0 / (D * HID), EPS, ALU.mult, ALU.add))
            v.tensor_scalar(theta[:], scaled[:, 5:7], 0.5, None, ALU.mult)
            link_pre(v.tensor_scalar(ntheta[:], scaled[:, 5:7], -0.5, None, ALU.mult))
            qk_lower(0, 1)
            bl = below.rearrange("p (k n) -> p k n", k=KD)
            link_pre(v.tensor_scalar(bl, fc_raw, ntheta[:, 0:1], None, ALU.is_lt))
            v.scalar_tensor_tensor(out=fc_t[:], in0=fc_raw, scalar=theta[:, 0:1], in1=bl,
                                   op0=ALU.is_gt, op1=ALU.subtract).then_inc(ternary_ready, 1)
            v_lower(0)
            dve.wait_ge(ternary_ready, 1)
            bl = below.rearrange("p (k n) -> p k n", k=NH)
            link_pre(v.tensor_scalar(bl, proj_raw, ntheta[:, 1:2], None, ALU.is_lt))
            v.scalar_tensor_tensor(out=proj_t32, in0=proj_raw, scalar=theta[:, 1:2], in1=bl,
                                   op0=ALU.is_gt, op1=ALU.subtract).then_inc(proj_t_ready, 1)
            dve.wait_ge(proj_t_ready, 1)
            v.tensor_copy(proj_t[:], proj_t32).then_inc(ternary_ready, 1)
            gelu_lower(0, 0)
            dve.wait_ge(crow_done, 1)
            v.tensor_copy(crow[:], small[0][0:1, :]).then_inc(crow_ready, 1)
            dve.wait_ge(csum_done, 1)
            v.tensor_copy(csum[:].rearrange("p a n -> p (a n)"), small[1][:]).then_inc(csum_ready, 1)
            for i in range(1, NF):
                gelu_lower(0, i)
            with dve.Fori(0, NB - 1) as b:
                both(b, True)
            both(NB - 1, False)

        @block.tensor
        def _(pe):
            mm = nc.tensor.matmul
            PARTS = ((0, 0), (0, 1), (1, 0))
            xt = (xt_hi, xt_lo)
            wt = (w_hi, w_lo)
            gt = (g_hi, g_lo)
            cts = (ct_hi, ct_lo)
            ps_hl = (p_hi, p_lo)

            def job(b, kind, n):
                ps = slot[kind, n]
                if kind == "xt":
                    wait(pe, b, xn_ready, 1)
                    for k in range(KD):
                        for t in range(NT):
                            last = nc.tensor.transpose(ps[:, k, t * P:(t + 1) * P], xn[:, t, k * P:(k + 1) * P],
                                                       ident[:])
                    last.then_inc(*sig(xt_done))
                elif kind == "qk":
                    if n == 0:
                        wait(pe, b, xt_ready, 1)
                    for m in range(KD):
                        i = 0
                        for k in range(KD):
                            for pw, px in PARTS:
                                last = mm(ps[:, m], wt[pw][:, n, k, m * P:(m + 1) * P], xt[px][:, k],
                                          start=(i == 0), stop=(i == 3 * KD - 1))
                                i += 1
                    last.then_inc(*sig(qk_done))
                elif kind == "v":
                    for t in range(NT):
                        i = 0
                        for k in range(KD):
                            for px, pw in PARTS:
                                last = mm(ps[:, t // 2, (t % 2) * D:(t % 2 + 1) * D],
                                          xt[px][:, k, t * P:(t + 1) * P], wt[pw][:, 2, k],
                                          start=(i == 0), stop=(i == 3 * KD - 1))
                                i += 1
                    last.then_inc(*sig(v_done))
                elif kind == "fc":
                    for a in range(2):
                        m = 2 * n + a
                        i = 0
                        for k in range(KD):
                            for px in range(2):
                                last = mm(ps[:, a], fc_t[:, k, m * P:(m + 1) * P], xt[px][:, k],
                                          start=(i == 0), stop=(i == 2 * KD - 1))
                                i += 1
                    last.then_inc(*sig(fc_done))
                elif kind == "sa":
                    if n == 0:
                        wait(pe, b, stacks_loaded, 16)
                    for a in range(2):
                        mm(ps[:, a], onehot[:], mask_q[:, 1 if n == 0 else 0].rearrange("p u k -> p (u k)"),
                           start=True, stop=False)
                        for u in range(4):
                            i = a * 4 + u
                            last = mm(ps[:, a, u * P:(u + 1) * P], q_stack[:, i, n],
                                      k_stack[:, i, n * W:n * W + P], start=False, stop=(u == 3))
                    last.then_inc(*sig(sa_done))
                elif kind == "mt":
                    wait(pe, b, max_ready, (n + 1) * HALF)
                    nc.tensor.transpose(ps[0:4 * NP, 0:P],
                                        negmax[:, n * HALF:(n + 1) * HALF].rearrange("p j u -> p (j u)"),
                                        ident[:]).then_inc(*sig(mt_done))
                elif kind == "st":
                    if n % HALF == 0:
                        wait(pe, b, shift_loaded[n // HALF], 3)
                    for a in range(2):
                        mm(ps[:, a], mask_k[:, 1 if n == 0 else 0], shift[:, n, a * 512:(a + 1) * 512],
                           start=True, stop=False)
                        for u in range(4):
                            i = a * 4 + u
                            last = mm(ps[:, a, u * P:(u + 1) * P], k_stack[:, i, n * W:n * W + P],
                                      q_stack[:, i, n], start=False, stop=(u == 3))
                    last.then_inc(*sig(st_done))
                elif kind == "mom":
                    wait(pe, b, halves_ready, 1)
                    for t in range(NT):
                        for c in range(2):
                            last = mm(ps[:, 2 * t + c:2 * t + c + 1], gsum2[:, c, t * P:(t + 1) * P],
                                      ones[:, 0:1], start=True, stop=True)
                    last.then_inc(*sig(mom_done))
                elif kind == "proj":
                    if n == 0:
                        wait(pe, b, g_ready, NH)
                    for i in range(NH):
                        for pg in range(2):
                            last = mm(ps[:, 0:D], gt[pg][:, i, n * P:(n + 1) * P], proj_t[:, i],
                                      start=(i == 0 and pg == 0), stop=(i == NH - 1 and pg == 1))
                    last.then_inc(*sig(proj_done))
                elif kind == "pv":
                    if n in ON_POOL:
                        wait(pe, b, p_lo_pool, ON_POOL.index(n) + 1)
                    else:
                        wait(pe, b, p_lo_dve, n + 1 - sum(j < n for j in ON_POOL))
                    if n == 0:
                        wait(pe, b, v_shifted, 4)
                    vals = v_odd if n % 2 == 0 else v_even
                    for i in range(NP):
                        for k, (pp, pw) in enumerate(PARTS):
                            last = mm(ps[:, i * VC:(i + 1) * VC], ps_hl[pp][:, n % PB, i], vals[:, pw, n // 2, i],
                                      start=(k == 0), stop=(k == 2))
                    last.then_inc(*sig(pv_done))
                elif kind == "ct":
                    wait(pe, b, ctx_ready, (n + 1) * HALF)
                    for i in range(HALF):
                        last = nc.tensor.transpose(ps[:, i * P:(i + 1) * P],
                                                   ctxn[:, n * HALF + i].rearrange("p u d -> p (u d)"), ident[:])
                    last.then_inc(*sig(ct_done))
                elif kind == "wo":
                    wait(pe, b, ct_ready, n // 2 + 1)
                    i = 0
                    for u in range(2):
                        for pc, pw in PARTS:
                            last = mm(ps[:, 0:D], cts[pc][:, u, n * P:(n + 1) * P], wt[pw][:, 3, u],
                                      start=(i == 0), stop=(i == 5))
                            i += 1
                    last.then_inc(*sig(wo_done))

            def run(b, order):
                for i, (kind, n) in enumerate(order):
                    wait_slot(pe, b, order, i)
                    job(b + 1 if (kind, n) in FRONT and order is not FRONT else b, kind, n)

            pe.wait_ge(pool_const, 3)
            for i, (kind, n) in enumerate(FRONT):
                if kind == "qk":
                    pe.wait_ge(w_ready, n + 1)
                if kind == "v":
                    pe.wait_ge(w_ready, 3)
                if kind == "fc" and n == 0:
                    pe.wait_ge(ternary_ready, 1)
                wait_slot(pe, 0, FRONT, i)
                job(0, kind, n)
            pe.wait_ge(consts_ready, 1)
            pe.wait_ge(proj_t_ready, 1)
            for c, vec in enumerate((lnw, lnb)):
                for i in range(NH):
                    last = mm(small[0][0:1, c * D:(c + 1) * D], vec[:, i:i + 1], proj_t32[:, i],
                              start=(i == 0), stop=(i == NH - 1))
            last.then_inc(crow_done, 1)
            pe.wait_ge(crow_ready, 1)
            mm(small[1][:], ones[0:1, :], crow[:], start=True, stop=True).then_inc(csum_done, 1)
            pe.wait_ge(csum_ready, 1)
            pe.wait_ge(ternary_ready, 2)
            pe.wait_ge(w_ready, 4)
            with pe.Fori(0, NB - 1) as b:
                run(b, BOTH)
            run(NB - 1, BACK)


_OUT_SHAPE = (8, 512, 256)


def kernel(**inputs):
    import numpy as _np
    import concourse.bacc as _bacc
    from concourse.bass_utils import run_bass_kernel_spmd as _run

    f = {k: _np.asarray(v) for k, v in inputs.items()}
    w_o = f["L0_attn_Wo"]

    def by_pair(w):
        return w.reshape(256, 8, 2, 16).transpose(0, 2, 3, 1).reshape(256, 256)

    laid = {
        "x": f["L0_attn_x"],
        "w_q": by_pair(f["L0_attn_Wq"]),
        "w_k": by_pair(f["L0_attn_Wk"]),
        "w_v": f["L0_attn_Wv"],
        "w_o": w_o.reshape(8, 2, 16, 256).transpose(1, 0, 2, 3).reshape(256, 256),
        "w_fc": f["L0_ffn_W_fc"].T,
        "ln_w": f["L0_ffn_ln_w"].reshape(8, 128).T,
        "ln_b": f["L0_ffn_ln_b"].reshape(8, 128).T,
        "w_proj": f["L0_ffn_W_proj"].T,
    }
    nc = _bacc.Bacc("TRN2", target_bir_lowering=False, num_devices=1)
    arrays, args = {}, []
    for name, a in laid.items():
        a = _np.ascontiguousarray(a)
        arrays[f"in_{name}"] = a
        args.append(nc.dram_tensor(f"in_{name}", a.shape, mybir.dt.from_np(a.dtype), kind="ExternalInput").ap())
    args.append(nc.dram_tensor("out_0", _OUT_SHAPE, mybir.dt.float32, kind="ExternalOutput").ap())
    attention_and_ternary_ffn(nc, *args)
    r = _run(nc, [arrays], core_ids=[0])
    return r.results[0]["out_0"]
```
